# Optimizing a Trainium2 kernel written in Bass

```python
import numpy as np
import jax
import jax.numpy as jnp

def _softmax(x, axis=-1):
    return jax.nn.softmax(x, axis=axis)

def _gelu(x):
    return jax.nn.gelu(x, approximate=True)

def _silu(x):
    return jax.nn.silu(x)

def _sigmoid(x):
    return jax.nn.sigmoid(x)

def _layernorm(x, axis=-1, eps=1e-05):
    m = jnp.mean(x, axis=axis, keepdims=True)
    v = jnp.var(x, axis=axis, keepdims=True)
    return (x - m) / jnp.sqrt(v + eps)

def _scatter_add(tgt, idx, src, axis=0):
    return tgt.at[idx].add(src)

def _segment_sum(src, seg, n):
    return jax.ops.segment_sum(src, seg, n)
kernel_name = 'mk_decoder_postln_d1_seqx_r4_70ca60'

def setup_inputs(seed: int=0):
    np.random.seed(seed)
    _w = jnp.asarray

    def _rec_inputs():
        import jax
        import jax.numpy as jnp
        _rk = jax.random.key(seed)
        x = 7.22e-05 + 1 * jax.random.normal(jax.random.fold_in(_rk, 1), (64, 256, 256), jnp.float32)
        _lenS = 256 - jax.random.randint(jax.random.fold_in(_rk, 7), (64,), 0, max(1, 256 // 4) + 1, jnp.int32)
        _lenS2 = 77 - jax.random.randint(jax.random.fold_in(_rk, 8), (64,), 0, max(1, 77 // 4) + 1, jnp.int32)
        _ctx_1024P = jax.random.normal(jax.random.fold_in(_rk, 11), (64, 16, 256), jnp.float32)
        _ctx_1024c = jax.random.dirichlet(jax.random.fold_in(_rk, 511), 0.3 * jnp.ones((16,), jnp.float32), (64, 77))
        _ctx_1024t = jnp.einsum('bsk,bkd->bsd', _ctx_1024c, _ctx_1024P)
        _ctx_1024t = _ctx_1024t * jax.lax.rsqrt(jnp.mean(jnp.square(_ctx_1024t)) + 1e-12) * 0.953939
        ctx_1024 = 4.13588e-05 + 0.999923 * (_ctx_1024t + 0.3 * jax.random.normal(jax.random.fold_in(_rk, 611), (64, 77, 256), jnp.float32))
        return (x, ctx_1024)
    x, ctx_1024 = _rec_inputs()

    def _L0_attn_setup():
        import jax, jax.numpy as jnp
        import numpy as np
        N_HEAD = 16
        key = jax.random.key(seed)
        ks = jax.random.split(key, 9)
        B, S, E = (2, 512, 256)
        sd = 1.0 / np.sqrt(E)
        inp = {'x': jax.random.normal(ks[0], (B, S, E), dtype=jnp.float32), 'Wq': jax.random.normal(ks[1], (E, E), dtype=jnp.float32) * sd, 'bq': jnp.zeros((E,), dtype=jnp.float32), 'Wk': jax.random.normal(ks[2], (E, E), dtype=jnp.float32) * sd, 'bk': jnp.zeros((E,), dtype=jnp.float32), 'Wv': jax.random.normal(ks[3], (E, E), dtype=jnp.float32) * sd, 'bv': jnp.zeros((E,), dtype=jnp.float32), 'Wp': jax.random.normal(ks[4], (E, E), dtype=jnp.float32) * sd, 'bp': jnp.zeros((E,), dtype=jnp.float32)}
        return inp
    _L0_attn_all = _L0_attn_setup()
    _L0_attn_in = {k: v for k, v in _L0_attn_all.items() if k in ('Wq', 'bq', 'Wk', 'bk', 'Wv', 'bv', 'Wp', 'bp')}
    del _L0_attn_all

    def _L0_xattn_setup():
        import jax, jax.numpy as jnp
        import numpy as np
        NEG_INF = 1000000000.0
        key = jax.random.key(seed)
        kq, kv = jax.random.split(key)
        B, T, D = (4, 512, 256)
        query = jax.random.normal(kq, (B, T, D), dtype=jnp.float32)
        value = jax.random.normal(kv, (B, T, D), dtype=jnp.float32)
        return {'query': query, 'value': value}
    _L0_xattn_all = _L0_xattn_setup()
    _L0_xattn_in = {k: v for k, v in _L0_xattn_all.items() if k in ()}
    del _L0_xattn_all

    def _L0_ffn_setup():
        import jax, jax.numpy as jnp
        import numpy as np
        EPS = 1e-05

        @jax.custom_vjp
        def ste_quantize(w):
            scale = jnp.maximum(jnp.mean(jnp.abs(w)), EPS)
            return jnp.clip(jnp.round(w / scale), -1.0, 1.0)

        def _ste_fwd(w):
            return (ste_quantize(w), None)

        def _ste_bwd(_, g):
            return (g,)
        ste_quantize.defvjp(_ste_fwd, _ste_bwd)
        key = jax.random.key(seed)
        k1, k2 = jax.random.split(key)
        x = jax.random.normal(k1, (8, 2048, 256), dtype=jnp.float32)
        weight = jax.random.normal(k2, (256, 256), dtype=jnp.float32) * 0.02
        return {'x': x, 'weight': weight}
    _L0_ffn_all = _L0_ffn_setup()
    _L0_ffn_in = {k: v for k, v in _L0_ffn_all.items() if k in ('weight',)}
    del _L0_ffn_all
    return {'x': x, 'ctx_1024': ctx_1024, 'L0_attn_Wq': _L0_attn_in['Wq'], 'L0_attn_bq': _L0_attn_in['bq'], 'L0_attn_Wk': _L0_attn_in['Wk'], 'L0_attn_bk': _L0_attn_in['bk'], 'L0_attn_Wv': _L0_attn_in['Wv'], 'L0_attn_bv': _L0_attn_in['bv'], 'L0_attn_Wp': _L0_attn_in['Wp'], 'L0_attn_bp': _L0_attn_in['bp'], 'L0_ffn_weight': _L0_ffn_in['weight']}

def reference(x, ctx_1024, L0_attn_Wq, L0_attn_bq, L0_attn_Wk, L0_attn_bk, L0_attn_Wv, L0_attn_bv, L0_attn_Wp, L0_attn_bp, L0_ffn_weight):
    import jax
    import jax.numpy as jnp

    def _L0_attn_ref(x, Wq, bq, Wk, bk, Wv, bv, Wp, bp):
        import jax, jax.numpy as jnp
        import numpy as np
        N_HEAD = 16
        B, S, E = x.shape
        H = N_HEAD
        D = E // H

        def split(h):
            return h.reshape(B, S, H, D).transpose(0, 2, 1, 3)
        q = split(x @ Wq.T + bq)
        k = split(x @ Wk.T + bk)
        v = split(x @ Wv.T + bv)
        scale = 1.0 / jnp.sqrt(jnp.asarray(D, dtype=x.dtype))
        attn = jnp.einsum('bhsd,bhtd->bhst', q, k) * scale
        causal = jnp.tril(jnp.ones((S, S), dtype=bool))
        attn = jnp.where(causal[None, None], attn, jnp.asarray(-jnp.inf, dtype=attn.dtype))
        attn = jax.nn.softmax(attn, axis=-1)
        y = jnp.einsum('bhst,bhtd->bhsd', attn, v)
        y = y.transpose(0, 2, 1, 3).reshape(B, S, E)
        return y @ Wp.T + bp

    def _L0_xattn_ref(query, value):
        import jax, jax.numpy as jnp
        import numpy as np
        NEG_INF = 1000000000.0
        k = value
        scores = jnp.einsum('bqd,bkd->bqk', query, k)
        Tq, Tv = (scores.shape[-2], scores.shape[-1])
        causal_mask = jnp.tril(jnp.ones((Tq, Tv), dtype=bool))
        scores = scores - NEG_INF * (~causal_mask).astype(scores.dtype)
        weights = jax.nn.softmax(scores, axis=-1)
        result = jnp.einsum('bqv,bvd->bqd', weights, value)
        return result

    def _L0_ffn_ref(x, weight):
        import jax, jax.numpy as jnp
        import numpy as np
        EPS = 1e-05

        @jax.custom_vjp
        def ste_quantize(w):
            scale = jnp.maximum(jnp.mean(jnp.abs(w)), EPS)
            return jnp.clip(jnp.round(w / scale), -1.0, 1.0)

        def _ste_fwd(w):
            return (ste_quantize(w), None)

        def _ste_bwd(_, g):
            return (g,)
        ste_quantize.defvjp(_ste_fwd, _ste_bwd)
        w_ternary = ste_quantize(weight)
        scale = jnp.maximum(jnp.mean(jnp.abs(weight)), EPS)
        return jnp.einsum('bsi,oi->bso', x, w_ternary * scale)
    x = _layernorm(x + _L0_attn_ref(x, L0_attn_Wq, L0_attn_bq, L0_attn_Wk, L0_attn_bk, L0_attn_Wv, L0_attn_bv, L0_attn_Wp, L0_attn_bp), axis=-1)
    x = _layernorm(x + _L0_xattn_ref(x, ctx_1024), axis=-1)
    x = _layernorm(x + _L0_ffn_ref(x, L0_ffn_weight), axis=-1)
    return x

_drawn_inputs = setup_inputs


def setup_inputs(seed=0):
    import zlib

    import numpy as np

    out = dict(_drawn_inputs(seed))
    spreads = {'L0_attn_bq': (0.0, 0.1),
     'L0_attn_bk': (0.0, 0.1),
     'L0_attn_bv': (0.0, 0.1),
     'L0_attn_bp': (0.0, 0.1)}
    factors = {}
    for name, (base, spread) in spreads.items():
        noise = np.random.default_rng([zlib.crc32(name.encode()), seed]).standard_normal(out[name].shape)
        drawn = base * np.exp(spread * noise) if base else spread * noise
        out[name] = jnp.asarray(drawn.astype(out[name].dtype))
    for name, factor in factors.items():
        out[name] = (out[name] * factor).astype(out[name].dtype)
    return out
```

```python
from contextlib import ExitStack

import concourse.bass as bass
from concourse import mybir

F32 = mybir.dt.float32
F32R = mybir.dt.float32r
BF16 = mybir.dt.bfloat16
ALU = mybir.AluOpType
ACT = mybir.ActivationFunctionType
AX = mybir.AxisListType

P = 128
HEADS = 16
DH = 16
QUADS = 4
PB = 2
SLOTS = 24
HW = 32
NPARTS = 6
KROWS = NPARTS * DH
LEAD = 10
NEG = -1.0e30
EPS = 1e-5


def decoder_layer(nc, x, ctx_in, wq, bq, wk, bk, wv, bv, wp, bp, wf, out):
    B, S, E = x.shape
    C = ctx_in.shape[1]
    NP = B // PB
    T = S // P
    KT = PB * T
    EC = E // P
    TOK = PB * S
    CP = 80
    SCALE = float(DH) ** -0.5
    assert (T, EC, KT, TOK, HEADS * DH) == (2, 2, 4, 512, E) and 6 * QUADS == SLOTS and NP >= 5

    x_tiles = x.rearrange("b (t p) d -> p (b t) d", p=P)
    out_tiles = out.rearrange("b (t p) d -> p (b t) d", p=P)
    ctx_rows = ctx_in.rearrange("b k d -> k b d")

    with ExitStack() as ctx:
        def sb(name, shape, dt=F32):
            return ctx.enter_context(nc.sbuf_tensor(name, shape, dt))

        def bank(name):
            return ctx.enter_context(nc.psum_tensor(name, [P, 512], F32))

        class Signal:

            def __init__(self, name, per, step=1):
                self.sem = ctx.enter_context(nc.semaphore(name))
                self.per, self.step = per, step

            def value(self, pair, k):
                return pair * (self.per * self.step) + k * self.step

        def need(eng, signal, pair, k):
            v = signal.value(pair, k)
            if isinstance(v, int) and v <= 0:
                return
            eng.wait_ge(signal.sem, v)

        def need_apart(eng, signal, pair, k):
            v = signal.value(pair, k)
            if isinstance(v, int):
                return need(eng, signal, pair, k)
            v = eng.to_reg(v)
            eng.wait_ge(cst, CONSTANTS)
            eng.wait_ge(signal.sem, v)

        ps_tail, ps_av, ps_head = bank("ps_tail"), bank("ps_av"), bank("ps_head")
        ps_max = [bank(f"ps_max{i}") for i in range(2)]
        ps_st = [bank(f"ps_st{i}") for i in range(3)]

        ident = sb("ident", [P, P])
        ident_b = sb("ident_b", [P, P], BF16)
        causal_b = sb("causal_b", [P, 4, P], BF16)
        xmask = sb("xmask", [P, KT, C])
        neg_half = sb("neg_half", [P, 2])
        ones = sb("ones", [P, P])
        w_raw = sb("w_raw", [P, 5, EC, E])
        wT_hi = [sb(f"wT_hi{i}", [P, EC, E], F32R) for i in range(4)]
        wT_lo = [sb(f"wT_lo{i}", [P, EC, E], F32R) for i in range(4)]
        wfT = sb("wfT", [P, EC, E], F32R)
        bqk = sb("bqk", [P, 2, EC])
        bv_col = sb("bv_col", [P, EC])
        bv_bc = sb("bv_bc", [P, EC, P])
        bp_row = sb("bp_row", [1, E])
        bias_bc = sb("bias_bc", [P, E])
        wf_abs = sb("wf_abs", [P, 1])
        fscale = sb("fscale", [P, 1])
        wf_half = sb("wf_half", [P, 2])
        wf_q = sb("wf_q", [P, EC, E])
        wf_n = sb("wf_n", [P, EC, E])

        xt = sb("xt", [P, KT, E])
        xT_hi = sb("xT_hi", [P, EC, TOK], F32R)
        xT_lo = sb("xT_lo", [P, EC, TOK], F32R)
        parts = [sb(f"parts{i}", [P, EC, NPARTS, TOK], BF16) for i in range(2)]
        rest = sb("rest", [P, TOK])
        stack = [sb(f"stack{i}", [P, HEADS, TOK], BF16) for i in range(2)]

        v_ext = sb("v_ext", [P, KT, HEADS, HW])
        rowmax = sb("rowmax", [P, 2, PB, T, 4])
        rowmax2 = sb("rowmax2", [P, 2, PB, 4])
        negmax = sb("negmax", [P, PB, T, 2, 4], BF16)
        negmax_t = sb("negmax_t", [8, TOK], BF16)
        probs = sb("probs", [P, 2, 6, 512])

        xres = sb("xres", [P, KT, E])
        ctx_sb = sb("ctx_sb", [C, PB, E])
        ctxT = sb("ctxT", [P, PB * EC, CP])
        y_sb = sb("y_sb", [P, QUADS, PB, S])
        rden = sb("rden", [P, KT, HEADS])
        yn = sb("yn", [P, KT, E])
        ynT_hi = sb("ynT_hi", [P, EC, TOK], F32R)
        ynT_lo = sb("ynT_lo", [P, EC, TOK], F32R)
        z = sb("z", [P, KT, E])
        bnst = sb("bnst", [P, KT, 6])
        mv = sb("mv", [P, KT, 2])
        vareps = sb("vareps", [P, KT])
        rstd = sb("rstd", [P, KT])
        h1 = sb("h1", [P, KT, E])
        h1T = sb("h1T", [P, EC, TOK])
        sc = sb("sc", [P, KT, C])
        nmx = sb("nmx", [P, KT])
        p2 = sb("p2", [P, KT, C])
        ssum = sb("ssum", [P, KT])
        rsum = sb("rsum", [P, KT])
        p2T = sb("p2T", [C, TOK])
        h2 = sb("h2", [P, KT, E])
        h2T_hi = sb("h2T_hi", [P, EC, TOK], F32R)
        h2T_lo = sb("h2T_lo", [P, EC, TOK], F32R)
        o_sb = sb("o_sb", [P, KT, E])

        W_IN = 16 * 9
        w_in = Signal("w_in", 1, W_IN)
        x_in = Signal("x_in", 1, 16)
        xres_in = Signal("xres_in", 1, 16)
        ctx_landed = Signal("ctx_landed", 1, 16)
        stack_in = [Signal(f"stack_in{q}", 8, 16) for q in range(QUADS)]
        mrow_in = [Signal(f"mrow_in{q}", 1, 16) for q in range(QUADS)]
        out_done = [Signal(f"out_done{b}", 1, 16) for b in range(PB)]
        mm_xT, mm_qk, mm_v = Signal("mm_xT", 2), Signal("mm_qk", 4), Signal("mm_v", 2)
        mm_mT, mm_ctxT = Signal("mm_mT", 4), Signal("mm_ctxT", 1)
        mm_max, mm_st, mm_av = Signal("mm_max", SLOTS), Signal("mm_st", SLOTS), Signal("mm_av", 4)
        mm_y, mm_ynT, mm_proj = Signal("mm_y", 4), Signal("mm_ynT", 2), Signal("mm_proj", 2)
        mm_h1T, mm_sc, mm_pT = Signal("mm_h1T", 2), Signal("mm_sc", 1), Signal("mm_pT", 1)
        mm_xav, mm_h2T, mm_ffn = Signal("mm_xav", 2), Signal("mm_h2T", 2), Signal("mm_ffn", 2)
        xT_hi_ok, qk_hi_ok, v_ok = Signal("xT_hi_ok", 2), Signal("qk_hi_ok", 4), Signal("v_ok", 2)
        ctxT_ok, exp_ok, y_ok = Signal("ctxT_ok", 1), Signal("exp_ok", SLOTS), Signal("y_ok", 4)
        ynT_hi_ok, h1T_ok = Signal("ynT_hi_ok", 2), Signal("h1T_ok", 2)
        p2_ok, p2T_ok, h2T_hi_ok = Signal("p2_ok", 1), Signal("p2T_ok", 1), Signal("h2T_hi_ok", 2)
        xT_lo_ok, rest_ok, parts_ok = Signal("xT_lo_ok", 2), Signal("rest_ok", 4), Signal("parts_ok", 4)
        max_ok, max2_ok, negmax_ok = Signal("max_ok", SLOTS), Signal("max2_ok", 4), Signal("negmax_ok", 4)
        neghi_ok, mT_ok = Signal("neghi_ok", 4), Signal("mT_ok", 4)
        rden_ok, yn_ok, ynT_lo_ok = Signal("rden_ok", 4), Signal("yn_ok", 4), Signal("ynT_lo_ok", 2)
        z_ok, stats_ok, mv_ok = Signal("z_ok", 6), Signal("stats_ok", 6), Signal("mv_ok", 6)
        var_ok, norm_ok = Signal("var_ok", 6), Signal("norm_ok", 6)
        sc_ok, nmx_ok, rsum_ok = Signal("sc_ok", 1), Signal("nmx_ok", 1), Signal("rsum_ok", 1)
        h2T_lo_ok = Signal("h2T_lo_ok", 2)
        sel_ok, low_ok = Signal("sel_ok", SLOTS), Signal("low_ok", 4)
        xres_ok, rstd_ok = Signal("xres_ok", 1), Signal("rstd_ok", 6)
        cst = ctx.enter_context(nc.semaphore("cst"))
        CONSTANTS = 9 + KT
        vcst = ctx.enter_context(nc.semaphore("vcst"))
        prep_mm = ctx.enter_context(nc.semaphore("prep_mm"))
        prep_hi = ctx.enter_context(nc.semaphore("prep_hi"))
        prep_lo = ctx.enter_context(nc.semaphore("prep_lo"))

        block = ctx.enter_context(nc.Block())

        def run(eng, iteration):
            iteration(-1, head=True)
            iteration(0, head=True, main=True)
            iteration(1, head=True, main=True, tail=True)
            with eng.Fori(2, NP - 1) as p:
                iteration(p, head=True, main=True, tail=True)
            iteration(NP - 1, main=True, tail=True)
            iteration(NP, tail=True)

        def max_unit(p, s, main, head):
            if s + LEAD < SLOTS:
                return (p, s + LEAD) if main else None
            return (p + 1, s + LEAD - SLOTS) if head else None

        MT_SLOT = {20: 0, 2: 1, 8: 2, 14: 3}
        STACK_SLOT = {10: 0, 16: 1, 20: 2, 4: 3}
        QK_SLOT = {7: (0, 0), 9: (0, 1), 15: (1, 0), 16: (1, 1)}

        @block.sync
        def _(sp):
            for i, w in enumerate((wq, wk, wv, wp, wf)):
                sp.dma_start(w_raw[:, i], w.rearrange("(c p) e -> p c e", p=P)).then_inc(w_in.sem, 16)
            with nc.allow_non_contiguous_dma(reason="biases by partition"):
                for i, b in enumerate((bq, bk)):
                    sp.dma_start(bqk[:, i, :], b.rearrange("(c p) -> p c", p=P)).then_inc(w_in.sem, 16)
                sp.dma_start(bv_col[:, :], bv.rearrange("(c p) -> p c", p=P)).then_inc(w_in.sem, 16)
            sp.dma_start(bp_row[:, :], bp.rearrange("(a e) -> a e", a=1)).then_inc(w_in.sem, 16)

            def copy_stack(q, pair):
                c = q // 2
                need_apart(sp, parts_ok, pair, 2 * c + 2)
                need_apart(sp, low_ok, pair, 2 * c + 2)
                need_apart(sp, mm_st, pair - 1, 6 * q + 6)
                for j in range(4):
                    h = 4 * q + j
                    r = h % 8
                    for i in range(2):
                        sp.dma_start(stack[i][0:KROWS, h, :], parts[i][DH * r:DH * r + DH, c, :, :])\
                            .then_inc(stack_in[q].sem, 16)

            def iteration(p, head=False, main=False, tail=False):
                for s in range(SLOTS):
                    if s == 0 and head:
                        need_apart(sp, mm_xT, p, 2)
                        sp.dma_start(xt[:, :, :], x_tiles[:, bass.ds((p + 1) * KT, KT), :])\
                            .then_inc(x_in.sem, 16)
                    if s == 0 and tail:
                        need_apart(sp, z_ok, p - 2, 2)
                        sp.dma_start(xres[:, :, :], x_tiles[:, bass.ds((p - 1) * KT, KT), :])\
                            .then_inc(xres_in.sem, 16)
                        need_apart(sp, mm_xav, p - 2, 2)
                        sp.dma_start(ctx_sb[:, :, :], ctx_rows[:, bass.ds((p - 1) * PB, PB), :])\
                            .then_inc(ctx_landed.sem, 16)
                    if s in MT_SLOT and (head if s == 20 else main):
                        q, pair = MT_SLOT[s], p + (s == 20)
                        need_apart(sp, mT_ok, pair, q + 1)
                        sp.dma_start(stack[0][KROWS:KROWS + 2, 4 * q:4 * q + 4, :], negmax_t[:, :])\
                            .then_inc(mrow_in[q].sem, 16)
                    if s in STACK_SLOT:
                        q = STACK_SLOT[s]
                        if q == 3 and main:
                            copy_stack(q, p)
                        if q < 3 and head:
                            copy_stack(q, p + 1)
                    if s == 23 and tail:
                        for b in range(PB):
                            need_apart(sp, norm_ok, p - 1, 5 + b)
                            sp.dma_start(out_tiles[:, bass.ds((p - 1) * KT + T * b, T), :],
                                         o_sb[:, T * b:T * b + T, :]).then_inc(out_done[b].sem, 16)

            run(sp, iteration)
            for b in range(PB):
                sp.wait_ge(out_done[b].sem, 16 * NP)

        @block.gpsimd
        def _(pool):
            pool.memset(ident[:, :], 0.0).then_inc(cst, 1)
            pool.memset(ident_b[:, :], 0.0).then_inc(cst, 1)
            pool.memset(causal_b[:, :, :], 0.0).then_inc(cst, 1)
            pool.memset(xmask[:, :, :], 0.0).then_inc(cst, 1)
            pool.memset(neg_half[:, :], -0.5).then_inc(cst, 1)
            pool.memset(ones[:, :], 1.0).then_inc(cst, 1)
            pool.wait_ge(cst, 6)
            for m in (ident, ident_b):
                pool.affine_select(out=m[:, :], in_=m[:, :], compare_op=ALU.not_equal, fill=1.0, base=0,
                                   pattern=[[-1, P]], channel_multiplier=1).then_inc(cst, 1)
            pool.affine_select(out=causal_b[:, :, :], in_=causal_b[:, :, :], compare_op=ALU.is_ge, fill=NEG,
                               base=0, pattern=[[0, 4], [-1, P]], channel_multiplier=1).then_inc(cst, 1)
            for b in range(PB):
                for t in range(T):
                    k = T * b + t
                    pool.affine_select(out=xmask[:, k, :], in_=xmask[:, k, :], compare_op=ALU.is_ge,
                                       fill=-1.0e9, base=P * t, pattern=[[-1, C]],
                                       channel_multiplier=1).then_inc(cst, 1)

            def iteration(p, head=False, main=False, tail=False):
                for s in range(SLOTS):
                    if main:
                        q, u = s // 6, s % 3
                        buf = probs[:, q % 2, s % 6, :]
                        n, w = (4, P) if u == 2 else (2, S)
                        part = buf.rearrange("p (j c) -> p j c", c=w)[:, :, 0:P]
                        need_apart(pool, exp_ok, p, s + 1)
                        pool.affine_select(out=part, in_=part, compare_op=ALU.is_ge, fill=0.0, base=0,
                                           pattern=[[0, n], [1, P]], channel_multiplier=-1)\
                            .then_inc(sel_ok.sem, 1)
                    if s == 1 and tail:
                        need(pool, xres_in, p - 1, 1)
                        if isinstance(p, int) and p == 1:
                            pool.wait_ge(prep_lo, 5)
                        pool.tensor_tensor(out=xres[:, :, :], in0=xres[:, :, :],
                                           in1=bias_bc[:, :].unsqueeze(1).to_broadcast([P, KT, E]),
                                           op=ALU.add).then_inc(xres_ok.sem, 1)
                    if s in QK_SLOT and head:
                        c, i = QK_SLOT[s]
                        n = 2 * c + i + 1
                        slot_m, slot_l = (3, 5) if i == 0 else (1, 2)
                        need(pool, parts_ok, p + 1, n)
                        pool.tensor_tensor(out=parts[i][:, c, slot_l, :], in0=rest[:, :],
                                           in1=parts[i][:, c, slot_m, :], op=ALU.subtract)\
                            .then_inc(low_ok.sem, 1)
                    ln = {9: 0, 10: 1, 17: 2, 18: 3, 22: 4, 23: 5}.get(s)
                    if ln is not None and tail:
                        b = ln % 2
                        need(pool, var_ok, p - 1, ln + 1)
                        pool.tensor_tensor(out=rstd[:, T * b:T * b + T], in0=vareps[:, T * b:T * b + T],
                                           in1=neg_half[:, :], op=ALU.pow).then_inc(rstd_ok.sem, 1)

            run(pool, iteration)

        @block.scalar
        def _(act):
            for i in range(5):
                act.wait_ge(prep_mm, i + 2)
                dst = wfT if i == 4 else wT_hi[i]
                act.activation(dst[:, :, :].rearrange("p c e -> p (c e)"), ps_tail[:, :] if i % 2 else ps_head[:, :],
                               ACT.Copy).then_inc(prep_hi, 1)

            def iteration(p, head=False, main=False, tail=False):
                for s in range(SLOTS):
                    if main:
                        q = s // 6
                        need(act, mm_st, p, s + 1)
                        need(act, mm_av, p, q - 1)
                        act.activation(probs[:, q % 2, s % 6, :], ps_st[s % 3][:, :], ACT.Exp,
                                       scale=SCALE).then_inc(exp_ok.sem, 1)
                    yq = {8: 0, 14: 1, 20: 2, 2: 3}.get(s)
                    if yq is not None and (tail if yq == 3 else main):
                        pair = p - (yq == 3)
                        need(act, mm_av, pair, yq + 1)
                        need(act, mm_y, pair - 1, 4)
                        act.activation(y_sb[:, yq, :, :].rearrange("p b s -> p (b s)"), ps_av[:, :],
                                       ACT.Copy).then_inc(y_ok.sem, 1)
                    if s in (3, 4) and main:
                        b = s - 3
                        need(act, mm_v, p, b + 1)
                        need(act, mm_av, p - 1, 4)
                        act.activation(v_ext[:, T * b:T * b + T, :, 0:DH],
                                       ps_head[:, :].rearrange("p (t h d) -> p t h d", t=T, d=DH),
                                       ACT.Copy).then_inc(v_ok.sem, 1)
                    if s in (5, 6) and head:
                        c = s - 5
                        need(act, mm_xT, p + 1, c + 1)
                        act.activation(xT_hi[:, c, :], ps_head[:, :], ACT.Copy).then_inc(xT_hi_ok.sem, 1)
                    if s in QK_SLOT and head:
                        c, i = QK_SLOT[s]
                        need(act, mm_qk, p + 1, 2 * c + i + 1)
                        for q in (2 * c, 2 * c + 1):
                            need(act, stack_in[q], p, 8)
                        act.activation(parts[i][:, c, 0, :], ps_head[:, :], ACT.Identity,
                                       bias=bqk[:, i, c:c + 1]).then_inc(qk_hi_ok.sem, 1)
                    if s in (7, 8) and tail:
                        c = s - 7
                        need(act, mm_ynT, p - 1, c + 1)
                        act.activation(ynT_hi[:, c, :], ps_tail[:, :], ACT.Copy).then_inc(ynT_hi_ok.sem, 1)
                    if s == 11 and tail:
                        need(act, mm_ctxT, p - 1, 1)
                        act.activation(ctxT[:, :, 0:C],
                                       ps_head[:, 0:PB * EC * CP].rearrange("p (n c) -> p n c", c=CP)[:, :, 0:C],
                                       ACT.Copy).then_inc(ctxT_ok.sem, 1)
                    if s in (12, 13) and tail:
                        c = s - 12
                        need(act, mm_h1T, p - 1, c + 1)
                        act.activation(h1T[:, c, :], ps_tail[:, :], ACT.Copy).then_inc(h1T_ok.sem, 1)
                    if s == 14 and tail:
                        need(act, nmx_ok, p - 1, 1)
                        need(act, rsum_ok, p - 2, 1)
                        for k in range(KT):
                            last = act.activation(p2[:, k, :], sc[:, k, :], ACT.Exp, bias=nmx[:, k:k + 1],
                                                  accum_out=ssum[:, k:k + 1])
                        last.then_inc(p2_ok.sem, 1)
                    if s == 16 and tail:
                        need(act, mm_pT, p - 1, 1)
                        act.activation(p2T[:, :], ps_tail[0:C, :], ACT.Copy).then_inc(p2T_ok.sem, 1)
                    if s in (20, 21) and tail:
                        c = s - 20
                        need(act, mm_h2T, p - 1, c + 1)
                        act.activation(h2T_hi[:, c, :], ps_tail[:, :], ACT.Copy).then_inc(h2T_hi_ok.sem, 1)

            run(act, iteration)

        @block.vector
        def _(dve):
            steps = [0]

            def step(ins):
                steps[0] += 1
                ins.then_inc(vcst, 1)
                dve.wait_ge(vcst, steps[0])

            dve.memset(v_ext[:, :, :, :], 0.0).then_inc(vcst, 1)
            dve.memset(stack[1][KROWS:KROWS + 2, :, :], 1.0).then_inc(vcst, 1)
            steps[0] = 2
            dve.wait_ge(vcst, 2)
            step(dve.memset(v_ext[:, :, :, DH:DH + 1], 1.0))
            dve.wait_ge(w_in.sem, W_IN)
            step(dve.tensor_reduce(wf_abs[:, :], w_raw[:, 4], axis=AX.XY, op=ALU.add,
                                   apply_absolute_value=True))
            dve.wait_ge(prep_mm, 1)
            step(dve.tensor_scalar(fscale[:, :], ps_av[:, 0:1], 1.0 / (E * E), EPS, ALU.mult, ALU.max))
            for i, half in enumerate((0.5, -0.5)):
                step(dve.tensor_scalar(wf_half[:, i:i + 1], fscale[:, :], half, None, ALU.mult))
            step(dve.tensor_scalar(wf_q[:, :, :], w_raw[:, 4], wf_half[:, 0:1], None, ALU.is_gt))
            step(dve.tensor_scalar(wf_n[:, :, :], w_raw[:, 4], wf_half[:, 1:2], None, ALU.is_lt))
            step(dve.tensor_tensor(out=wf_q[:, :, :], in0=wf_q[:, :, :], in1=wf_n[:, :, :], op=ALU.subtract))
            for c in range(EC):
                step(dve.tensor_scalar(bv_bc[:, c, :], ones[:, :], bv_col[:, c:c + 1], None, ALU.mult))
            for i in range(4):
                dve.wait_ge(prep_hi, i + 1)
                dve.tensor_tensor(out=wT_lo[i][:, :, :].rearrange("p c e -> p (c e)"),
                                  in0=ps_tail[:, :] if i % 2 else ps_head[:, :],
                                  in1=wT_hi[i][:, :, :].rearrange("p c e -> p (c e)").bitcast(F32),
                                  op=ALU.subtract).then_inc(prep_lo, 1)
            dve.wait_ge(prep_mm, 7)
            dve.tensor_copy(bias_bc[:, :], ps_av[:, 0:E]).then_inc(prep_lo, 1)

            def layernorm(pair, n, b, dst):
                need(dve, z_ok, pair, n)
                for k in (T * b, T * b + 1):
                    last = dve.bn_stats(bnst[:, k, :], z[:, k, :])
                last.then_inc(stats_ok.sem, 1)
                need_apart(dve, stats_ok, pair, n)
                for k in (T * b, T * b + 1):
                    last = dve.bn_aggr(mv[:, k, :], bnst[:, k, :])
                last.then_inc(mv_ok.sem, 1)
                need(dve, mv_ok, pair, n)
                dve.tensor_scalar(vareps[:, T * b:T * b + T], mv[:, T * b:T * b + T, 1], EPS, None,
                                  ALU.add).then_inc(var_ok.sem, 1)

            def normalize(pair, n, b, dst):
                need(dve, rstd_ok, pair, n)
                for k in (T * b, T * b + 1):
                    last = dve.tensor_scalar(dst[:, k, :], z[:, k, :], mv[:, k, 0:1], rstd[:, k:k + 1],
                                             ALU.subtract, ALU.mult)
                last.then_inc(norm_ok.sem, 1)

            def iteration(p, head=False, main=False, tail=False):
                for s in range(SLOTS):
                    unit = max_unit(p, s, main, head)
                    if unit:
                        pair, n = unit
                        q, b, u = n // 6, n // 3 % 2, n % 3
                        need(dve, mm_max, pair, n + 1)
                        dve.tensor_reduce(rowmax2[:, q % 2, b, :] if u == 2 else rowmax[:, q % 2, b, u, :],
                                          ps_max[n % 2][:, :].rearrange("p (j c) -> p j c", c=P),
                                          axis=AX.X, op=ALU.max).then_inc(max_ok.sem, 1)
                        if n % 6 == 5:
                            need(dve, max_ok, pair, n + 1)
                            m = rowmax[:, q % 2]
                            dve.tensor_tensor(out=m[:, :, 1, :], in0=m[:, :, 1, :], in1=rowmax2[:, q % 2],
                                              op=ALU.max).then_inc(max2_ok.sem, 1)
                            need(dve, max2_ok, pair, q + 1)
                            need(dve, mm_mT, pair, q)
                            mx = m.rearrange("p b t j -> p (b t) j")
                            hi, lo = (negmax[:, :, :, i, :].rearrange("p b t j -> p (b t) j") for i in range(2))
                            dve.tensor_scalar(hi, mx, -1.0, None, ALU.mult).then_inc(neghi_ok.sem, 1)
                            need(dve, neghi_ok, pair, q + 1)
                            dve.scalar_tensor_tensor(out=lo, in0=mx, scalar=-1.0, in1=hi, op0=ALU.mult,
                                                     op1=ALU.subtract).then_inc(negmax_ok.sem, 1)
                    if s in MT_SLOT and (head if s == 20 else main):
                        q, pair = MT_SLOT[s], p + (s == 20)
                        need(dve, mm_mT, pair, q + 1)
                        need(dve, mrow_in[(q - 1) % 4], pair - (q == 0), 1)
                        dve.tensor_copy(negmax_t[:, :], ps_head[:, :].bitcast(BF16)[0:8, 0:TOK])\
                            .then_inc(mT_ok.sem, 1)
                    if s in (5, 6) and head:
                        c = s - 5
                        need(dve, xT_hi_ok, p + 1, c + 1)
                        dve.tensor_tensor(out=xT_lo[:, c, :], in0=ps_head[:, :],
                                          in1=xT_hi[:, c, :].bitcast(F32), op=ALU.subtract)\
                            .then_inc(xT_lo_ok.sem, 1)
                    if s in QK_SLOT and head:
                        c, i = QK_SLOT[s]
                        n = 2 * c + i + 1
                        need(dve, qk_hi_ok, p + 1, n)
                        need(dve, low_ok, p + 1, n - 1)
                        dve.scalar_tensor_tensor(out=rest[:, :], in0=ps_head[:, :], scalar=bqk[:, i, c:c + 1],
                                                 in1=parts[i][:, c, 0, :], op0=ALU.add, op1=ALU.subtract)\
                            .then_inc(rest_ok.sem, 1)
                        pt = parts[i][:, c]
                        hi2, mid2 = (pt[:, 1:3], pt[:, 3:5]) if i == 0 else (pt[:, 3:6:2], pt[:, 1:5:3])
                        dve.tensor_copy(hi2, pt[:, 0:1].to_broadcast([P, 2, TOK]))
                        need(dve, rest_ok, p + 1, n)
                        dve.tensor_copy(mid2, rest[:, :].unsqueeze(1).to_broadcast([P, 2, TOK]))\
                            .then_inc(parts_ok.sem, 1)
                    if 3 <= s < 7 and tail:
                        k = s - 3
                        need(dve, mm_y, p - 1, k + 1)
                        y3 = ps_tail[:, :].rearrange("p (h d) -> p h d", d=HW)
                        dve.reciprocal(rden[:, k, :].unsqueeze(2), y3[:, :, DH:DH + 1]).then_inc(rden_ok.sem, 1)
                        need(dve, rden_ok, p - 1, k + 1)
                        dve.tensor_tensor(out=yn[:, k, :].rearrange("p (h d) -> p h d", d=DH),
                                          in0=y3[:, :, 0:DH],
                                          in1=rden[:, k, :].unsqueeze(2).to_broadcast([P, HEADS, DH]),
                                          op=ALU.mult).then_inc(yn_ok.sem, 1)
                    if s in (7, 8) and tail:
                        c = s - 7
                        need(dve, ynT_hi_ok, p - 1, c + 1)
                        dve.tensor_tensor(out=ynT_lo[:, c, :], in0=ps_tail[:, :],
                                          in1=ynT_hi[:, c, :].bitcast(F32), op=ALU.subtract)\
                            .then_inc(ynT_lo_ok.sem, 1)
                    if s in (9, 10) and tail:
                        b = s - 9
                        if b == 1:
                            normalize(p - 1, 1, 0, h1)
                        need(dve, mm_proj, p - 1, b + 1)
                        need(dve, xres_ok, p - 1, 1)
                        dve.tensor_tensor(out=z[:, T * b:T * b + T, :].rearrange("p t e -> p (t e)"),
                                          in0=ps_tail[:, :],
                                          in1=xres[:, T * b:T * b + T, :].rearrange("p t e -> p (t e)"),
                                          op=ALU.add).then_inc(z_ok.sem, 1)
                        layernorm(p - 1, b + 1, b, h1)
                    if s == 11 and tail:
                        normalize(p - 1, 2, 1, h1)
                    if s == 14 and tail:
                        need(dve, mm_sc, p - 1, 1)
                        dve.tensor_tensor(out=sc[:, :, :],
                                          in0=ps_tail[:, 0:KT * CP].rearrange("p (k c) -> p k c", c=CP)[:, :, 0:C],
                                          in1=xmask[:, :, :], op=ALU.add).then_inc(sc_ok.sem, 1)
                        need(dve, sc_ok, p - 1, 1)
                        dve.tensor_reduce(nmx[:, :], sc[:, :, :], axis=AX.X, op=ALU.max, negate=True)\
                            .then_inc(nmx_ok.sem, 1)
                    if s == 16 and tail:
                        need(dve, p2_ok, p - 1, 1)
                        dve.reciprocal(rsum[:, :], ssum[:, :]).then_inc(rsum_ok.sem, 1)
                    if s in (17, 18) and tail:
                        b = s - 17
                        if b == 1:
                            normalize(p - 1, 3, 0, h2)
                        need(dve, mm_xav, p - 1, b + 1)
                        need(dve, rsum_ok, p - 1, 1)
                        for k in (T * b, T * b + 1):
                            last = dve.scalar_tensor_tensor(out=z[:, k, :], in0=ps_tail[:, (k % T) * E:(k % T + 1) * E],
                                                            scalar=rsum[:, k:k + 1], in1=h1[:, k, :],
                                                            op0=ALU.mult, op1=ALU.add)
                        last.then_inc(z_ok.sem, 1)
                        layernorm(p - 1, b + 3, b, h2)
                    if s == 19 and tail:
                        normalize(p - 1, 4, 1, h2)
                    if s in (20, 21) and tail:
                        c = s - 20
                        need(dve, h2T_hi_ok, p - 1, c + 1)
                        dve.tensor_tensor(out=h2T_lo[:, c, :], in0=ps_tail[:, :],
                                          in1=h2T_hi[:, c, :].bitcast(F32), op=ALU.subtract)\
                            .then_inc(h2T_lo_ok.sem, 1)
                    if s in (22, 23) and tail:
                        b = s - 22
                        if b == 1:
                            need(dve, out_done[0], p - 2, 1)
                            normalize(p - 1, 5, 0, o_sb)
                        need(dve, mm_ffn, p - 1, b + 1)
                        for k in (T * b, T * b + 1):
                            last = dve.scalar_tensor_tensor(out=z[:, k, :], in0=ps_tail[:, (k % T) * E:(k % T + 1) * E],
                                                            scalar=fscale[:, 0:1], in1=h2[:, k, :],
                                                            op0=ALU.mult, op1=ALU.add)
                        last.then_inc(z_ok.sem, 1)
                        layernorm(p - 1, b + 5, b, o_sb)
                        if b == 1:
                            need(dve, out_done[1], p - 2, 1)
                            normalize(p - 1, 6, 1, o_sb)

            run(dve, iteration)

        @block.tensor
        def _(pe):
            def three_passes(dst, st_hi, st_lo, mv_hi, mv_lo, chunks):
                n = 0
                for c in range(chunks):
                    for a, m in ((st_hi, mv_hi), (st_hi, mv_lo), (st_lo, mv_hi)):
                        last = pe.matmul(dst, a(c), m(c), start=(n == 0), stop=(n == 3 * chunks - 1))
                        n += 1
                return last

            pe.wait_ge(cst, 8)
            pe.wait_ge(vcst, 4)
            pe.matmul(ps_av[:, 0:1], ones[:, :], wf_abs[:, :], start=True, stop=True).then_inc(prep_mm, 1)
            pe.wait_ge(w_in.sem, W_IN)

            def transpose_weights(i, src):
                dst = ps_tail if i % 2 else ps_head
                for ci in range(EC):
                    for co in range(EC):
                        last = pe.transpose(dst[:, ci * E + co * P:ci * E + co * P + P],
                                            src[:, co, ci * P:(ci + 1) * P], ident[:, :])
                last.then_inc(prep_mm, 1)

            for i in range(4):
                if i >= 2:
                    pe.wait_ge(prep_lo, i - 1)
                transpose_weights(i, w_raw[:, i])
            pe.wait_ge(vcst, 12)
            pe.wait_ge(prep_lo, 4)
            transpose_weights(4, wf_q)
            n = 0
            for c in range(EC):
                for part in (wT_hi[3], wT_lo[3]):
                    pe.matmul(ps_av[:, 0:E], bv_bc[:, c, :], part[:, c, :].bitcast(F32), start=(n == 0), stop=False)
                    n += 1
            pe.matmul(ps_av[:, 0:E], ones[0:1, :], bp_row[:, :], start=False, stop=True).then_inc(prep_mm, 1)
            pe.wait_ge(prep_hi, 5)
            pe.wait_ge(prep_lo, 5)

            def iteration(p, head=False, main=False, tail=False):
                for s in range(SLOTS):
                    if main:
                        q, b, u = s // 6, s // 3 % 2, s % 3
                        if s % 6 == 0:
                            need(pe, mrow_in[q], p, 1)
                        need(pe, exp_ok, p, s - 2)
                        t0 = b * S
                        for j in (range(4) if u == 2 else range(2 * u, 2 * u + 2)):
                            h = 4 * q + j
                            if u == 2:
                                keys, queries, at = slice(t0 + P, t0 + S), slice(t0 + P, t0 + S), P * j
                            else:
                                keys, queries, at = slice(t0, t0 + P), slice(t0, t0 + S), S * (j % 2)
                            last = pe.matmul(ps_st[s % 3][:, at:at + queries.stop - queries.start],
                                             stack[1][0:KROWS + 2, h, keys], stack[0][0:KROWS + 2, h, queries],
                                             start=True, stop=True)
                        last.then_inc(mm_st.sem, 1)
                    unit = max_unit(p, s, main, head)
                    if unit:
                        pair, n = unit
                        q, b, u = n // 6, n // 3 % 2, n % 3
                        if n % 6 == 0:
                            need(pe, stack_in[q], pair, 8)
                        need(pe, max_ok, pair, n - 1)
                        t0 = b * S
                        queries = slice(t0, t0 + P) if u == 0 else slice(t0 + P, t0 + S)
                        keys = slice(t0 + P, t0 + S) if u == 2 else slice(t0, t0 + P)
                        if u != 1:
                            pe.matmul(ps_max[n % 2][:, :], ident_b[:, :],
                                      causal_b[:, :, :].rearrange("p j c -> p (j c)"), start=True, stop=False)
                        for j in range(4):
                            h = 4 * q + j
                            last = pe.matmul(ps_max[n % 2][:, P * j:P * j + P], stack[0][0:KROWS, h, queries],
                                             stack[1][0:KROWS, h, keys], start=(u == 1), stop=(u == 1 or j == 3))
                        last.then_inc(mm_max.sem, 1)
                    av = {5: (0, 0), 8: (0, 1), 11: (1, 0), 14: (1, 1), 17: (2, 0), 20: (2, 1), 23: (3, 0),
                          2: (3, 1)}.get(s)
                    if av and (tail if s == 2 else main):
                        q, b = av
                        pair = p - (s == 2)
                        need(pe, sel_ok, pair, 6 * q + 3 * b + 3)
                        if q == 0:
                            need(pe, v_ok, pair, b + 1)
                        if b == 0:
                            need(pe, y_ok, pair, q)
                        for kb in range(T):
                            for j in range(4):
                                if kb == 0:
                                    pr = probs[:, q % 2, 3 * b + j // 2, S * (j % 2):S * (j % 2) + S]
                                else:
                                    pr = probs[:, q % 2, 3 * b + 2, P * j:P * j + P]
                                last = pe.matmul(ps_av[HW * j:HW * j + HW, b * S + kb * P:b * S + S],
                                                 v_ext[:, T * b + kb, 4 * q + j, :], pr,
                                                 start=(kb == 0), stop=(kb == 1), skip_group_check=True,
                                                 tile_position=(0, HW * j))
                        if b == 1:
                            last.then_inc(mm_av.sem, 1)
                    if s in MT_SLOT and (head if s == 20 else main):
                        q, pair = MT_SLOT[s], p + (s == 20)
                        need(pe, negmax_ok, pair, q + 1)
                        if s == 20:
                            need(pe, parts_ok, pair, 4)
                        elif s == 2:
                            need(pe, mT_ok, p, 1)
                        elif s == 8 and head:
                            need(pe, rest_ok, p + 1, 1)
                        elif s == 8:
                            need(pe, v_ok, p, 2)
                        elif s == 14 and head:
                            need(pe, rest_ok, p + 1, 2)
                        elif s == 14:
                            need(pe, mT_ok, p, 3)
                        if s == 14 and tail:
                            need(pe, ctxT_ok, p - 1, 1)
                        for b in range(PB):
                            for t in range(T):
                                at = (T * b + t) * P
                                last = pe.transpose(ps_head[:, :].bitcast(BF16)[0:8, at:at + P],
                                                    negmax[:, b, t, :, :].rearrange("p i j -> p (i j)"), ident_b[:, :])
                        last.then_inc(mm_mT.sem, 1)
                    if s in (3, 4) and main:
                        b = s - 3
                        if b == 0:
                            need(pe, mT_ok, p, 2)
                            need(pe, xT_lo_ok, p, 2)
                        else:
                            need(pe, v_ok, p, 1)
                        for t in range(T):
                            tok = slice((T * b + t) * P, (T * b + t + 1) * P)
                            last = three_passes(ps_head[:, t * E:(t + 1) * E],
                                                lambda c: xT_hi[:, c, tok], lambda c: xT_lo[:, c, tok],
                                                lambda c: wT_hi[2][:, c, :], lambda c: wT_lo[2][:, c, :], EC)
                        last.then_inc(mm_v.sem, 1)
                    if s in (5, 6) and head:
                        c = s - 5
                        if c == 0:
                            need(pe, x_in, p + 1, 1)
                            if main:
                                need(pe, v_ok, p, 2)
                        else:
                            need(pe, xT_lo_ok, p + 1, 1)
                        for k in range(KT):
                            last = pe.transpose(ps_head[:, k * P:(k + 1) * P], xt[:, k, c * P:(c + 1) * P],
                                                ident[:, :])
                        last.then_inc(mm_xT.sem, 1)
                    if s in QK_SLOT and head:
                        c, i = QK_SLOT[s]
                        if s == 7:
                            need(pe, xT_lo_ok, p + 1, 2)
                        elif s == 9:
                            need(pe, rest_ok, p + 1, 1)
                            if main:
                                need(pe, mT_ok, p, 3)
                        elif s == 15:
                            need(pe, rest_ok, p + 1, 2)
                            if main:
                                need(pe, mT_ok, p, 4)
                        else:
                            need(pe, rest_ok, p + 1, 3)
                        out_c = slice(c * P, (c + 1) * P)
                        three_passes(ps_head[:, :],
                                     lambda k: wT_hi[i][:, k, out_c], lambda k: wT_lo[i][:, k, out_c],
                                     lambda k: xT_hi[:, k, :], lambda k: xT_lo[:, k, :], EC)\
                            .then_inc(mm_qk.sem, 1)
                    if s == 11 and tail:
                        need(pe, ctx_landed, p - 1, 1)
                        if head:
                            need(pe, rest_ok, p + 1, 2)
                        elif main:
                            need(pe, mT_ok, p, 3)
                        for b in range(PB):
                            for c in range(EC):
                                n = b * EC + c
                                last = pe.transpose(ps_head[:, n * CP:n * CP + C],
                                                    ctx_sb[:, b, c * P:(c + 1) * P], ident[0:C, 0:C])
                        last.then_inc(mm_ctxT.sem, 1)
                    if 3 <= s < 7 and tail:
                        k = s - 3
                        b, t = k // T, k % T
                        if k == 0:
                            need(pe, y_ok, p - 1, 4)
                            need(pe, z_ok, p - 2, 6)
                        else:
                            need(pe, yn_ok, p - 1, k)
                        for q in range(QUADS):
                            last = pe.transpose(ps_tail[:, q * P:(q + 1) * P], y_sb[:, q, b, t * P:(t + 1) * P],
                                                ident[:, :])
                        last.then_inc(mm_y.sem, 1)
                    if s in (7, 8) and tail:
                        c = s - 7
                        if c == 0:
                            need(pe, yn_ok, p - 1, 4)
                        else:
                            need(pe, ynT_lo_ok, p - 1, 1)
                        for k in range(KT):
                            last = pe.transpose(ps_tail[:, k * P:(k + 1) * P], yn[:, k, c * P:(c + 1) * P],
                                                ident[:, :])
                        last.then_inc(mm_ynT.sem, 1)
                    if s in (9, 10) and tail:
                        b = s - 9
                        if b == 0:
                            need(pe, ynT_lo_ok, p - 1, 2)
                        else:
                            need(pe, z_ok, p - 1, 1)
                        for t in range(T):
                            tok = slice((T * b + t) * P, (T * b + t + 1) * P)
                            last = three_passes(ps_tail[:, t * E:(t + 1) * E],
                                                lambda c: ynT_hi[:, c, tok], lambda c: ynT_lo[:, c, tok],
                                                lambda c: wT_hi[3][:, c, :], lambda c: wT_lo[3][:, c, :], EC)
                        last.then_inc(mm_proj.sem, 1)
                    if s in (12, 13) and tail:
                        c = s - 12
                        if c == 0:
                            need(pe, norm_ok, p - 1, 2)
                        else:
                            need(pe, h1T_ok, p - 1, 1)
                        for k in range(KT):
                            last = pe.transpose(ps_tail[:, k * P:(k + 1) * P], h1[:, k, c * P:(c + 1) * P],
                                                ident[:, :])
                        last.then_inc(mm_h1T.sem, 1)
                    if s == 14 and tail:
                        need(pe, h1T_ok, p - 1, 2)
                        need(pe, ctxT_ok, p - 1, 1)
                        for k in range(KT):
                            for c in range(EC):
                                last = pe.matmul(ps_tail[:, k * CP:k * CP + C], h1T[:, c, k * P:(k + 1) * P],
                                                 ctxT[:, (k // T) * EC + c, 0:C], start=(c == 0), stop=(c == EC - 1))
                        last.then_inc(mm_sc.sem, 1)
                    if s == 16 and tail:
                        need(pe, p2_ok, p - 1, 1)
                        for k in range(KT):
                            last = pe.transpose(ps_tail[0:C, k * P:(k + 1) * P], p2[:, k, :], ident[:, :])
                        last.then_inc(mm_pT.sem, 1)
                    if s in (17, 18) and tail:
                        b = s - 17
                        if b == 0:
                            need(pe, p2T_ok, p - 1, 1)
                        else:
                            need(pe, z_ok, p - 1, 3)
                        for t in range(T):
                            k = T * b + t
                            last = pe.matmul(ps_tail[:, t * E:(t + 1) * E], p2T[:, k * P:(k + 1) * P],
                                             ctx_sb[:, b, :], start=True, stop=True)
                        last.then_inc(mm_xav.sem, 1)
                    if s in (20, 21) and tail:
                        c = s - 20
                        if c == 0:
                            need(pe, norm_ok, p - 1, 4)
                        else:
                            need(pe, h2T_lo_ok, p - 1, 1)
                        for k in range(KT):
                            last = pe.transpose(ps_tail[:, k * P:(k + 1) * P], h2[:, k, c * P:(c + 1) * P],
                                                ident[:, :])
                        last.then_inc(mm_h2T.sem, 1)
                    if s in (22, 23) and tail:
                        b = s - 22
                        if b == 0:
                            need(pe, h2T_lo_ok, p - 1, 2)
                        else:
                            need(pe, z_ok, p - 1, 5)
                        for t in range(T):
                            tok = slice((T * b + t) * P, (T * b + t + 1) * P)
                            n = 0
                            for c in range(EC):
                                for a in (h2T_hi, h2T_lo):
                                    last = pe.matmul(ps_tail[:, t * E:(t + 1) * E], a[:, c, tok], wfT[:, c, :],
                                                     start=(n == 0), stop=(n == 2 * EC - 1))
                                    n += 1
                        last.then_inc(mm_ffn.sem, 1)

            run(pe, iteration)


_INS = ["x", "ctx_1024", "L0_attn_Wq", "L0_attn_bq", "L0_attn_Wk", "L0_attn_bk", "L0_attn_Wv", "L0_attn_bv",
        "L0_attn_Wp", "L0_attn_bp", "L0_ffn_weight"]


def kernel(**inputs):
    import numpy as _np
    import concourse.bacc as _bacc
    from concourse import mybir as _mybir
    from concourse.bass_utils import run_bass_kernel_spmd as _run

    nc = _bacc.Bacc("TRN2", target_bir_lowering=False, num_devices=1)
    arrays, args = {}, []
    for name in _INS:
        a = _np.ascontiguousarray(inputs[name])
        arrays[f"in_{name}"] = a
        args.append(nc.dram_tensor(f"in_{name}", a.shape, _mybir.dt.from_np(a.dtype), kind="ExternalInput").ap())
    shape = inputs["x"].shape
    args.append(nc.dram_tensor("out_0", shape, _mybir.dt.float32, kind="ExternalOutput").ap())
    decoder_layer(nc, *args)
    r = _run(nc, [arrays], core_ids=[0])
    return r.results[0]["out_0"]
```

```python
from contextlib import ExitStack

import concourse.bass as bass
from concourse import mybir

F32 = mybir.dt.float32
F32R = mybir.dt.float32r
BF16 = mybir.dt.bfloat16
ALU = mybir.AluOpType
ACT = mybir.ActivationFunctionType
AX = mybir.AxisListType

P = 128
HEADS = 16
DH = 16
QUADS = 4
PB = 2
SLOTS = 24
HW = 32
NPARTS = 6
KROWS = NPARTS * DH
LEAD = 10
NEG = -1.0e30
EPS = 1e-5


def decoder_layer(nc, x, ctx_in, wq, bq, wk, bk, wv, bv, wp, bp, wf, out):
    B, S, E = x.shape
    C = ctx_in.shape[1]
    NP = B // PB
    T = S // P
    KT = PB * T
    EC = E // P
    TOK = PB * S
    CP = 80
    SCALE = float(DH) ** -0.5
    assert (T, EC, KT, TOK, HEADS * DH) == (2, 2, 4, 512, E) and 6 * QUADS == SLOTS and NP >= 5

    x_tiles = x.rearrange("b (t p) d -> p (b t) d", p=P)
    out_tiles = out.rearrange("b (t p) d -> p (b t) d", p=P)
    ctx_rows = ctx_in.rearrange("b k d -> k b d")

    with ExitStack() as ctx:
        def sb(name, shape, dt=F32):
            return ctx.enter_context(nc.sbuf_tensor(name, shape, dt))

        def bank(name):
            return ctx.enter_context(nc.psum_tensor(name, [P, 512], F32))

        class Signal:

            def __init__(self, name, per, step=1):
                self.sem = ctx.enter_context(nc.semaphore(name))
                self.per, self.step = per, step

            def value(self, pair, k):
                return pair * (self.per * self.step) + k * self.step

        def need(eng, signal, pair, k):
            v = signal.value(pair, k)
            if isinstance(v, int) and v <= 0:
                return
            eng.wait_ge(signal.sem, v)

        def need_apart(eng, signal, pair, k):
            v = signal.value(pair, k)
            if isinstance(v, int):
                return need(eng, signal, pair, k)
            v = eng.to_reg(v)
            eng.wait_ge(cst, CONSTANTS)
            eng.wait_ge(signal.sem, v)

        ps_av, ps_head = bank("ps_av"), bank("ps_head")
        ps_tail, ps_max, ps_st = ([bank(f"{n}{i}") for i in range(2)] for n in ("ps_tail", "ps_max", "ps_st"))

        ident = sb("ident", [P, P])
        ident_b = sb("ident_b", [P, P], BF16)
        causal_b = sb("causal_b", [P, 4, P], BF16)
        xmask = sb("xmask", [P, KT, C])
        neg_half = sb("neg_half", [P, KT])
        ones = sb("ones", [P, P])
        w_raw = sb("w_raw", [P, 5, EC, E])
        wT_hi = [sb(f"wT_hi{i}", [P, EC, E], F32R) for i in range(4)]
        wT_lo = [sb(f"wT_lo{i}", [P, EC, E], F32R) for i in range(4)]
        wfT = sb("wfT", [P, EC, E], F32R)
        bqk = sb("bqk", [P, 2, EC])
        bv_col = sb("bv_col", [P, EC])
        bv_bc = sb("bv_bc", [P, EC, P])
        bp_row = sb("bp_row", [1, E])
        bias_bc = sb("bias_bc", [P, E])
        wf_abs = sb("wf_abs", [P, 1])
        fscale = sb("fscale", [P, 1])
        wf_half = sb("wf_half", [P, 2])

        xt = sb("xt", [P, KT, E])
        xT_hi = sb("xT_hi", [P, EC, TOK], F32R)
        xT_lo = sb("xT_lo", [P, EC, TOK], F32R)
        parts = [sb(f"parts{i}", [P, EC, NPARTS, TOK], BF16) for i in range(2)]
        rest = sb("rest", [P, 2, TOK])
        stack = [sb(f"stack{i}", [P, HEADS, TOK], BF16) for i in range(2)]

        v_ext = sb("v_ext", [P, KT, HEADS, HW])
        rowmax = sb("rowmax", [P, 2, PB, T, 4])
        rowmax2 = sb("rowmax2", [P, 2, PB, 4])
        negmax = sb("negmax", [P, PB, T, 2, 4], BF16)
        negmax_t = sb("negmax_t", [8, TOK], BF16)
        probs = sb("probs", [P, 2, 6, 512])

        xres = sb("xres", [P, KT, E])
        ctx_sb = sb("ctx_sb", [C, PB, E])
        ctxT = sb("ctxT", [P, PB * EC, CP])
        y_sb = sb("y_sb", [P, QUADS, PB, S])
        rden = sb("rden", [P, KT, HEADS])
        yn = sb("yn", [P, KT, E])
        ynT_hi = sb("ynT_hi", [P, EC, TOK], F32R)
        ynT_lo = sb("ynT_lo", [P, EC, TOK], F32R)
        zs = [sb(f"z{i}", [P, KT, E]) for i in range(2)]
        bnst = sb("bnst", [P, KT, 6])
        mv = sb("mv", [P, KT, 2])
        vareps = sb("vareps", [P, KT])
        negmean = sb("negmean", [P, KT])
        rstd = sb("rstd", [P, KT])
        shift = sb("shift", [P, KT])
        h1 = sb("h1", [P, KT, E])
        h1T = sb("h1T", [P, EC, TOK])
        sc = sb("sc", [P, KT, C])
        nmx = sb("nmx", [P, KT])
        p2 = sb("p2", [P, KT, C])
        ssum = sb("ssum", [P, KT])
        rsum = sb("rsum", [P, KT])
        p2T = sb("p2T", [C, TOK])
        h2 = sb("h2", [P, KT, E])
        h2T_hi = sb("h2T_hi", [P, EC, TOK], F32R)
        h2T_lo = sb("h2T_lo", [P, EC, TOK], F32R)
        o_sb = sb("o_sb", [P, KT, E])

        wf_q, wf_n = h1[:, 0:EC, :], h1[:, EC:2 * EC, :]

        W_IN = 16 * 9
        w_in = Signal("w_in", 1, W_IN)
        x_in = Signal("x_in", 1, 16)
        xres_in = Signal("xres_in", 1, 16)
        ctx_landed = Signal("ctx_landed", 1, 16)
        stack_in = [Signal(f"stack_in{q}", 8, 16) for q in range(QUADS)]
        mrow_in = [Signal(f"mrow_in{q}", 1, 16) for q in range(QUADS)]
        out_done = [Signal(f"out_done{b}", 1, 16) for b in range(PB)]
        mm_xT, mm_qk, mm_v = Signal("mm_xT", 2), Signal("mm_qk", 4), Signal("mm_v", 2)
        mm_mT, mm_ctxT = Signal("mm_mT", 4), Signal("mm_ctxT", 1)
        mm_max, mm_st, mm_av = Signal("mm_max", SLOTS), Signal("mm_st", SLOTS), Signal("mm_av", 8)
        mm_y, mm_ynT, mm_proj = Signal("mm_y", 4), Signal("mm_ynT", 2), Signal("mm_proj", 2)
        mm_h1T, mm_sc, mm_pT = Signal("mm_h1T", 2), Signal("mm_sc", 1), Signal("mm_pT", 1)
        mm_xav, mm_h2T, mm_ffn = Signal("mm_xav", 2), Signal("mm_h2T", 2), Signal("mm_ffn", 2)
        xT_hi_ok, qk_hi_ok, v_ok = Signal("xT_hi_ok", 2), Signal("qk_hi_ok", 4), Signal("v_ok", 2)
        ctxT_ok, exp_ok, y_ok = Signal("ctxT_ok", 1), Signal("exp_ok", SLOTS), Signal("y_ok", 4)
        ynT_hi_ok, h1T_ok = Signal("ynT_hi_ok", 2), Signal("h1T_ok", 2)
        p2_ok, p2T_ok, h2T_hi_ok = Signal("p2_ok", 1), Signal("p2T_ok", 1), Signal("h2T_hi_ok", 2)
        mid_ok, mT_ok = Signal("mid_ok", 4), Signal("mT_ok", 4)
        xT_lo_ok, rest_ok, copies_ok = Signal("xT_lo_ok", 2), Signal("rest_ok", 4), Signal("copies_ok", 4)
        max_ok, max2_ok, negmax_ok = Signal("max_ok", SLOTS), Signal("max2_ok", 4), Signal("negmax_ok", 4)
        neghi_ok = Signal("neghi_ok", 4)
        rden_ok, yn_ok, ynT_lo_ok = Signal("rden_ok", 4), Signal("yn_ok", 4), Signal("ynT_lo_ok", 2)
        z_ok, stats_ok, mv_ok = Signal("z_ok", 6), Signal("stats_ok", 3), Signal("mv_ok", 3)
        var_ok, norm_ok = Signal("var_ok", 3), Signal("norm_ok", 6)
        sc_ok, nmx_ok, rsum_ok = Signal("sc_ok", 1), Signal("nmx_ok", 1), Signal("rsum_ok", 1)
        h2T_lo_ok = Signal("h2T_lo_ok", 2)
        sel_ok, low_ok, xres_ok = Signal("sel_ok", SLOTS), Signal("low_ok", 4), Signal("xres_ok", 1)
        rstd_ok, shift_ok = Signal("rstd_ok", 3), Signal("shift_ok", 3)
        cst = ctx.enter_context(nc.semaphore("cst"))
        CONSTANTS = 9 + KT
        vcst = ctx.enter_context(nc.semaphore("vcst"))
        prep_mm = ctx.enter_context(nc.semaphore("prep_mm"))
        prep_hi = ctx.enter_context(nc.semaphore("prep_hi"))
        prep_lo = ctx.enter_context(nc.semaphore("prep_lo"))

        block = ctx.enter_context(nc.Block())

        def run(eng, iteration):
            iteration(-1, load=True, head=True)
            iteration(0, load=True, head=True, main=True)
            iteration(1, load=True, head=True, main=True, tail=True)
            iteration(2, load=True, head=True, main=True, tail=True, late=True)
            with eng.Fori(3, NP - 2) as p:
                iteration(p, load=True, head=True, main=True, tail=True, late=True)
            iteration(NP - 2, head=True, main=True, tail=True, late=True)
            iteration(NP - 1, main=True, tail=True, late=True)
            iteration(NP, tail=True, late=True)
            iteration(NP + 1, late=True)

        def max_unit(p, s, main, head):
            if s + LEAD < SLOTS:
                return (p, s + LEAD) if main else None
            return (p + 1, s + LEAD - SLOTS) if head else None

        MT_SLOT = {21: 0, 3: 1, 9: 2, 15: 3}
        STACK_SLOT = {10: 0, 12: 1, 18: 2, 0: 3}
        X_SLOT, RES_SLOT, BIAS_SLOT = 5, 0, 4
        XT_SLOT = {3: 0, 4: 1}
        QK_SLOT = {6: (0, 0), 7: (0, 1), 15: (1, 0), 16: (1, 1)}
        V_SLOT, V_READ_SLOT = {0: 0, 2: 1}, {0: 0, 2: 1}
        HEADS_SLOT = {7: (0, 1), 8: (2, 3)}
        YNT_SLOT, PROJ_SLOT, CTXT_SLOT = 10, {12: 0, 13: 1}, 13
        STATS_SLOT, POW_SLOT = {13: 0, 22: 1, 29: 2}, {14: 0, 23: 1, 30: 2}
        NORM_SLOT = {14: (0, 0), 15: (0, 1), 23: (1, 0), 24: (1, 1), 31: (2, 0), 35: (2, 1)}
        H1T_SLOT, SCORE_SLOT, SOFTMAX_SLOT, PT_SLOT, XAV_SLOT = 16, 17, 19, 20, 22
        H2T_SLOT, FFN_SLOT, STORE_SLOT = 25, {27: 0, 28: 1}, 35

        def stages(p, s, tail, late):
            return [(p - 2, s + SLOTS)] * late + [(p - 1, s)] * tail

        HI, HI_COPIES = (0, 2), (slice(1, 3), slice(3, 5))
        MID, MIDS, LOW = (3, 0), (slice(3, 6, 2), slice(0, 6, 5)), (4, 1)

        @block.sync
        def _(sp):
            sp.dma_start(xt[:, :, :], x_tiles[:, 0:KT, :]).then_inc(x_in.sem, 16)
            for i, w in enumerate((wq, wk, wv, wp, wf)):
                sp.dma_start(w_raw[:, i], w.rearrange("(c p) e -> p c e", p=P)).then_inc(w_in.sem, 16)
            with nc.allow_non_contiguous_dma(reason="biases by partition"):
                for i, b in enumerate((bq, bk)):
                    sp.dma_start(bqk[:, i, :], b.rearrange("(c p) -> p c", p=P)).then_inc(w_in.sem, 16)
                sp.dma_start(bv_col[:, :], bv.rearrange("(c p) -> p c", p=P)).then_inc(w_in.sem, 16)
            sp.dma_start(bp_row[:, :], bp.rearrange("(a e) -> a e", a=1)).then_inc(w_in.sem, 16)

            def copy_stack(q, pair):
                c = q // 2
                need_apart(sp, copies_ok, pair, 2 * c + 2)
                need_apart(sp, low_ok, pair, 2 * c + 2)
                need_apart(sp, mm_st, pair - 1, 6 * q + 6)
                for j in range(4):
                    h = 4 * q + j
                    r = h % 8
                    for i in range(2):
                        sp.dma_start(stack[i][0:KROWS, h, :], parts[i][DH * r:DH * r + DH, c, :, :])\
                            .then_inc(stack_in[q].sem, 16)

            def iteration(p, load=False, head=False, main=False, tail=False, late=False):
                for s in range(SLOTS):
                    if s == X_SLOT and load:
                        need_apart(sp, mm_xT, p + 1, 2)
                        sp.dma_start(xt[:, :, :], x_tiles[:, bass.ds((p + 2) * KT, KT), :])\
                            .then_inc(x_in.sem, 16)
                    if s == RES_SLOT and tail:
                        need_apart(sp, z_ok, p - 2, 2)
                        sp.dma_start(xres[:, :, :], x_tiles[:, bass.ds((p - 1) * KT, KT), :])\
                            .then_inc(xres_in.sem, 16)
                        need_apart(sp, mm_xav, p - 2, 2)
                        sp.dma_start(ctx_sb[:, :, :], ctx_rows[:, bass.ds((p - 1) * PB, PB), :])\
                            .then_inc(ctx_landed.sem, 16)
                    if s in MT_SLOT and (head if s == 21 else main):
                        q, pair = MT_SLOT[s], p + (s == 21)
                        need_apart(sp, mT_ok, pair, q + 1)
                        sp.dma_start(stack[0][KROWS:KROWS + 2, 4 * q:4 * q + 4, :], negmax_t[:, :])\
                            .then_inc(mrow_in[q].sem, 16)
                    if s in STACK_SLOT:
                        q = STACK_SLOT[s]
                        if q == 3 and main:
                            copy_stack(q, p)
                        if q < 3 and head:
                            copy_stack(q, p + 1)
                    for pair, a in stages(p, s, tail, late):
                        if a == STORE_SLOT:
                            for b in range(PB):
                                need_apart(sp, norm_ok, pair, 5 + b)
                                sp.dma_start(out_tiles[:, bass.ds(pair * KT + T * b, T), :],
                                             o_sb[:, T * b:T * b + T, :]).then_inc(out_done[b].sem, 16)

            run(sp, iteration)
            for b in range(PB):
                sp.wait_ge(out_done[b].sem, 16 * NP)

        @block.gpsimd
        def _(pool):
            pool.memset(ident[:, :], 0.0).then_inc(cst, 1)
            pool.memset(ident_b[:, :], 0.0).then_inc(cst, 1)
            pool.memset(causal_b[:, :, :], 0.0).then_inc(cst, 1)
            pool.memset(xmask[:, :, :], 0.0).then_inc(cst, 1)
            pool.memset(neg_half[:, :], -0.5).then_inc(cst, 1)
            pool.memset(ones[:, :], 1.0).then_inc(cst, 1)
            pool.wait_ge(cst, 6)
            for m in (ident, ident_b):
                pool.affine_select(out=m[:, :], in_=m[:, :], compare_op=ALU.not_equal, fill=1.0, base=0,
                                   pattern=[[-1, P]], channel_multiplier=1).then_inc(cst, 1)
            pool.affine_select(out=causal_b[:, :, :], in_=causal_b[:, :, :], compare_op=ALU.is_ge, fill=NEG,
                               base=0, pattern=[[0, 4], [-1, P]], channel_multiplier=1).then_inc(cst, 1)
            for b in range(PB):
                for t in range(T):
                    k = T * b + t
                    pool.affine_select(out=xmask[:, k, :], in_=xmask[:, k, :], compare_op=ALU.is_ge,
                                       fill=-1.0e9, base=P * t, pattern=[[-1, C]],
                                       channel_multiplier=1).then_inc(cst, 1)

            def iteration(p, load=False, head=False, main=False, tail=False, late=False):
                for s in range(SLOTS):
                    if main:
                        q, u = s // 6, s % 3
                        buf = probs[:, q % 2, s % 6, :]
                        n, w = (4, P) if u == 2 else (2, S)
                        part = buf.rearrange("p (j c) -> p j c", c=w)[:, :, 0:P]
                        need_apart(pool, exp_ok, p, s + 1)
                        pool.affine_select(out=part, in_=part, compare_op=ALU.is_ge, fill=0.0, base=0,
                                           pattern=[[0, n], [1, P]], channel_multiplier=-1)\
                            .then_inc(sel_ok.sem, 1)
                    if s == BIAS_SLOT and tail:
                        need(pool, xres_in, p - 1, 1)
                        if isinstance(p, int) and p == 1:
                            pool.wait_ge(prep_lo, 5)
                        pool.tensor_tensor(out=xres[:, :, :], in0=xres[:, :, :],
                                           in1=bias_bc[:, :].unsqueeze(1).to_broadcast([P, KT, E]),
                                           op=ALU.add).then_inc(xres_ok.sem, 1)
                    if s - 2 in QK_SLOT and head:
                        c, i = QK_SLOT[s - 2]
                        n = 2 * c + i + 1
                        need(pool, mid_ok, p + 1, n)
                        pool.tensor_tensor(out=parts[i][:, c, LOW[i], :], in0=rest[:, i, :],
                                           in1=parts[i][:, c, MID[i], :], op=ALU.subtract)\
                            .then_inc(low_ok.sem, 1)
                    for pair, a in stages(p, s, tail, late):
                        if a in POW_SLOT:
                            ln = POW_SLOT[a]
                            need(pool, var_ok, pair, ln + 1)
                            pool.tensor_tensor(out=rstd[:, :], in0=vareps[:, :], in1=neg_half[:, :],
                                               op=ALU.pow).then_inc(rstd_ok.sem, 1)
                            need(pool, rstd_ok, pair, ln + 1)
                            pool.tensor_tensor(out=shift[:, :], in0=negmean[:, :], in1=rstd[:, :],
                                               op=ALU.mult).then_inc(shift_ok.sem, 1)

            run(pool, iteration)

        @block.scalar
        def _(act):
            for i in range(5):
                act.wait_ge(prep_mm, i + 2)
                dst = wfT if i == 4 else wT_hi[i]
                act.activation(dst[:, :, :].rearrange("p c e -> p (c e)"), ps_tail[0][:, :] if i % 2 else ps_head[:, :],
                               ACT.Copy).then_inc(prep_hi, 1)

            def normalize(pair, ln, b, dst):
                need(act, shift_ok, pair, ln + 1)
                for k in (T * b, T * b + 1):
                    last = act.activation(dst[:, k, :], zs[ln % 2][:, k, :], ACT.Identity, bias=shift[:, k:k + 1],
                                          scale=rstd[:, k:k + 1])
                last.then_inc(norm_ok.sem, 1)

            def after_attention(pair, a):
                if a in NORM_SLOT:
                    ln, b = NORM_SLOT[a]
                    if ln == 2:
                        need(act, out_done[b], pair - 1, 1)
                    normalize(pair, ln, b, (h1, h2, o_sb)[ln])
                if a == YNT_SLOT:
                    for c in range(EC):
                        need(act, mm_ynT, pair, c + 1)
                        act.activation(ynT_hi[:, c, :], ps_tail[c][:, :], ACT.Copy).then_inc(ynT_hi_ok.sem, 1)
                if a == CTXT_SLOT:
                    need(act, mm_ctxT, pair, 1)
                    act.activation(ctxT[:, :, 0:C],
                                   ps_tail[0][:, 0:PB * EC * CP].rearrange("p (n c) -> p n c", c=CP)[:, :, 0:C],
                                   ACT.Copy).then_inc(ctxT_ok.sem, 1)
                if a == H1T_SLOT:
                    for c in range(EC):
                        need(act, mm_h1T, pair, c + 1)
                        act.activation(h1T[:, c, :], ps_tail[c][:, :], ACT.Copy).then_inc(h1T_ok.sem, 1)
                if a == SOFTMAX_SLOT:
                    need(act, nmx_ok, pair, 1)
                    need(act, rsum_ok, pair - 1, 1)
                    for k in range(KT):
                        last = act.activation(p2[:, k, :], sc[:, k, :], ACT.Exp, bias=nmx[:, k:k + 1],
                                              accum_out=ssum[:, k:k + 1])
                    last.then_inc(p2_ok.sem, 1)
                if a == PT_SLOT:
                    need(act, mm_pT, pair, 1)
                    act.activation(p2T[:, :], ps_tail[1][0:C, :], ACT.Copy).then_inc(p2T_ok.sem, 1)
                if a == H2T_SLOT:
                    for c in range(EC):
                        need(act, mm_h2T, pair, c + 1)
                        act.activation(h2T_hi[:, c, :], ps_tail[c][:, :], ACT.Copy).then_inc(h2T_hi_ok.sem, 1)

            def iteration(p, load=False, head=False, main=False, tail=False, late=False):
                for s in range(SLOTS):
                    if main:
                        q = s // 6
                        need(act, mm_st, p, s + 1)
                        need(act, mm_av, p, 2 * q - 2)
                        act.activation(probs[:, q % 2, s % 6, :], ps_st[s % 2][:, :], ACT.Exp,
                                       scale=SCALE).then_inc(exp_ok.sem, 1)
                    if s - 1 in QK_SLOT and head:
                        c, i = QK_SLOT[s - 1]
                        n = 2 * c + i + 1
                        need(act, rest_ok, p + 1, n)
                        act.activation(parts[i][:, c, MIDS[i], :], rest[:, i:i + 1, :].to_broadcast([P, 2, TOK]),
                                       ACT.Copy).then_inc(mid_ok.sem, 1)
                    yq = {8: 0, 14: 1, 20: 2, 2: 3}.get(s)
                    if yq is not None and (tail if yq == 3 else main):
                        pair = p - (yq == 3)
                        need(act, mm_av, pair, 2 * yq + 2)
                        need(act, mm_y, pair - 1, 4)
                        act.activation(y_sb[:, yq, :, :].rearrange("p b s -> p (b s)"), ps_av[:, :],
                                       ACT.Copy).then_inc(y_ok.sem, 1)
                    if s in MT_SLOT and (head if s == 21 else main):
                        q, pair = MT_SLOT[s], p + (s == 21)
                        need(act, mm_mT, pair, q + 1)
                        need(act, mrow_in[(q - 1) % 4], pair - (q == 0), 1)
                        act.activation(negmax_t[:, :], ps_av[:, :].bitcast(BF16)[0:8, 0:TOK], ACT.Copy)\
                            .then_inc(mT_ok.sem, 1)
                    for pair, a in stages(p, s, tail, late):
                        after_attention(pair, a)
                    if s in XT_SLOT and head:
                        c = XT_SLOT[s]
                        need(act, mm_xT, p + 1, c + 1)
                        act.activation(xT_hi[:, c, :], ps_head[:, :], ACT.Copy).then_inc(xT_hi_ok.sem, 1)
                    if s in QK_SLOT and head:
                        c, i = QK_SLOT[s]
                        n = 2 * c + i + 1
                        need(act, mm_qk, p + 1, n)
                        for q in (2 * c, 2 * c + 1):
                            need(act, stack_in[q], p, 8)
                        act.activation(parts[i][:, c, HI[i], :], ps_head[:, :], ACT.Identity,
                                       bias=bqk[:, i, c:c + 1]).then_inc(qk_hi_ok.sem, 1)
                    if s in V_READ_SLOT and main:
                        b = V_READ_SLOT[s]
                        need(act, mm_v, p, b + 1)
                        need(act, mm_av, p - 1, 7 + b)
                        act.activation(v_ext[:, T * b:T * b + T, :, 0:DH].rearrange("p t h d -> p (t h) d"),
                                       ps_head[:, :].rearrange("p (n d) -> p n d", d=DH),
                                       ACT.Copy).then_inc(v_ok.sem, 1)

            run(act, iteration)

        @block.vector
        def _(dve):
            steps = [0]

            def step(ins):
                steps[0] += 1
                ins.then_inc(vcst, 1)
                dve.wait_ge(vcst, steps[0])

            dve.memset(v_ext[:, :, :, :], 0.0).then_inc(vcst, 1)
            dve.memset(stack[1][KROWS:KROWS + 2, :, :], 1.0).then_inc(vcst, 1)
            steps[0] = 2
            dve.wait_ge(vcst, 2)
            step(dve.memset(v_ext[:, :, :, DH:DH + 1], 1.0))
            dve.wait_ge(w_in.sem, W_IN)
            step(dve.tensor_reduce(wf_abs[:, :], w_raw[:, 4], axis=AX.XY, op=ALU.add,
                                   apply_absolute_value=True))
            dve.wait_ge(prep_mm, 1)
            step(dve.tensor_scalar(fscale[:, :], ps_av[:, 0:1], 1.0 / (E * E), EPS, ALU.mult, ALU.max))
            for i, half in enumerate((0.5, -0.5)):
                step(dve.tensor_scalar(wf_half[:, i:i + 1], fscale[:, :], half, None, ALU.mult))
            step(dve.tensor_scalar(wf_q, w_raw[:, 4], wf_half[:, 0:1], None, ALU.is_gt))
            step(dve.tensor_scalar(wf_n, w_raw[:, 4], wf_half[:, 1:2], None, ALU.is_lt))
            step(dve.tensor_tensor(out=wf_q, in0=wf_q, in1=wf_n, op=ALU.subtract))
            for c in range(EC):
                step(dve.tensor_scalar(bv_bc[:, c, :], ones[:, :], bv_col[:, c:c + 1], None, ALU.mult))
            for i in range(4):
                dve.wait_ge(prep_hi, i + 1)
                dve.tensor_tensor(out=wT_lo[i][:, :, :].rearrange("p c e -> p (c e)"),
                                  in0=ps_tail[0][:, :] if i % 2 else ps_head[:, :],
                                  in1=wT_hi[i][:, :, :].rearrange("p c e -> p (c e)").bitcast(F32),
                                  op=ALU.subtract).then_inc(prep_lo, 1)
            dve.wait_ge(prep_mm, 7)
            dve.tensor_copy(bias_bc[:, :], ps_av[:, 0:E]).then_inc(prep_lo, 1)

            def statistics(pair, ln):
                for b in range(PB):
                    need(dve, z_ok, pair, 2 * ln + 1 + b)
                    for k in (T * b, T * b + 1):
                        last = dve.bn_stats(bnst[:, k, :], zs[ln % 2][:, k, :])
                last.then_inc(stats_ok.sem, 1)
                need_apart(dve, stats_ok, pair, ln + 1)
                for k in range(KT):
                    last = dve.bn_aggr(mv[:, k, :], bnst[:, k, :])
                last.then_inc(mv_ok.sem, 1)
                need(dve, mv_ok, pair, ln + 1)
                dve.tensor_scalar(vareps[:, :], mv[:, :, 1], EPS, None, ALU.add)
                dve.tensor_scalar(negmean[:, :], mv[:, :, 0], -1.0, None, ALU.mult).then_inc(var_ok.sem, 1)

            def after_attention(pair, a):
                if a == H2T_SLOT:
                    for c in range(EC):
                        need(dve, h2T_hi_ok, pair, c + 1)
                        dve.tensor_tensor(out=h2T_lo[:, c, :], in0=ps_tail[c][:, :],
                                          in1=h2T_hi[:, c, :].bitcast(F32), op=ALU.subtract)\
                            .then_inc(h2T_lo_ok.sem, 1)
                if a in FFN_SLOT:
                    b = FFN_SLOT[a]
                    need(dve, mm_ffn, pair, b + 1)
                    for k in (T * b, T * b + 1):
                        last = dve.scalar_tensor_tensor(
                            out=zs[0][:, k, :], in0=ps_tail[b][:, (k % T) * E:(k % T + 1) * E],
                            scalar=fscale[:, 0:1], in1=h2[:, k, :], op0=ALU.mult, op1=ALU.add)
                    last.then_inc(z_ok.sem, 1)
                if a in HEADS_SLOT:
                    for k in HEADS_SLOT[a]:
                        need(dve, mm_y, pair, k + 1)
                        y3 = ps_tail[k % 2][:, :].rearrange("p (h d) -> p h d", d=HW)
                        dve.reciprocal(rden[:, k, :].unsqueeze(2), y3[:, :, DH:DH + 1])\
                            .then_inc(rden_ok.sem, 1)
                        need(dve, rden_ok, pair, k + 1)
                        dve.tensor_tensor(out=yn[:, k, :].rearrange("p (h d) -> p h d", d=DH),
                                          in0=y3[:, :, 0:DH],
                                          in1=rden[:, k, :].unsqueeze(2).to_broadcast([P, HEADS, DH]),
                                          op=ALU.mult).then_inc(yn_ok.sem, 1)
                if a == YNT_SLOT:
                    for c in range(EC):
                        need(dve, ynT_hi_ok, pair, c + 1)
                        dve.tensor_tensor(out=ynT_lo[:, c, :], in0=ps_tail[c][:, :],
                                          in1=ynT_hi[:, c, :].bitcast(F32), op=ALU.subtract)\
                            .then_inc(ynT_lo_ok.sem, 1)
                if a in PROJ_SLOT:
                    b = PROJ_SLOT[a]
                    need(dve, mm_proj, pair, b + 1)
                    need(dve, xres_ok, pair, 1)
                    need(dve, norm_ok, pair - 1, 6)
                    dve.tensor_tensor(out=zs[0][:, T * b:T * b + T, :].rearrange("p t e -> p (t e)"),
                                      in0=ps_tail[b][:, :],
                                      in1=xres[:, T * b:T * b + T, :].rearrange("p t e -> p (t e)"),
                                      op=ALU.add).then_inc(z_ok.sem, 1)
                if a == SCORE_SLOT:
                    need(dve, mm_sc, pair, 1)
                    dve.tensor_tensor(out=sc[:, :, :],
                                      in0=ps_tail[0][:, 0:KT * CP].rearrange("p (k c) -> p k c", c=CP)[:, :, 0:C],
                                      in1=xmask[:, :, :], op=ALU.add).then_inc(sc_ok.sem, 1)
                    need(dve, sc_ok, pair, 1)
                    dve.tensor_reduce(nmx[:, :], sc[:, :, :], axis=AX.X, op=ALU.max, negate=True)\
                        .then_inc(nmx_ok.sem, 1)
                if a == PT_SLOT:
                    need(dve, p2_ok, pair, 1)
                    dve.reciprocal(rsum[:, :], ssum[:, :]).then_inc(rsum_ok.sem, 1)
                if a == XAV_SLOT:
                    need(dve, rsum_ok, pair, 1)
                    for b in range(PB):
                        need(dve, mm_xav, pair, b + 1)
                        for k in (T * b, T * b + 1):
                            last = dve.scalar_tensor_tensor(
                                out=zs[1][:, k, :], in0=ps_tail[b][:, (k % T) * E:(k % T + 1) * E],
                                scalar=rsum[:, k:k + 1], in1=h1[:, k, :], op0=ALU.mult, op1=ALU.add)
                        last.then_inc(z_ok.sem, 1)
                if a in STATS_SLOT:
                    statistics(pair, STATS_SLOT[a])

            def iteration(p, load=False, head=False, main=False, tail=False, late=False):
                for s in range(SLOTS):
                    unit = max_unit(p, s, main, head)
                    if unit:
                        pair, n = unit
                        q, b, u = n // 6, n // 3 % 2, n % 3
                        need(dve, mm_max, pair, n + 1)
                        dve.tensor_reduce(rowmax2[:, q % 2, b, :] if u == 2 else rowmax[:, q % 2, b, u, :],
                                          ps_max[n % 2][:, :].rearrange("p (j c) -> p j c", c=P),
                                          axis=AX.X, op=ALU.max).then_inc(max_ok.sem, 1)
                        if n % 6 == 5:
                            need(dve, max_ok, pair, n + 1)
                            m = rowmax[:, q % 2]
                            dve.tensor_tensor(out=m[:, :, 1, :], in0=m[:, :, 1, :], in1=rowmax2[:, q % 2],
                                              op=ALU.max).then_inc(max2_ok.sem, 1)
                            need(dve, max2_ok, pair, q + 1)
                            need(dve, mm_mT, pair, q)
                            mx = m.rearrange("p b t j -> p (b t) j")
                            hi, lo = (negmax[:, :, :, i, :].rearrange("p b t j -> p (b t) j") for i in range(2))
                            dve.tensor_scalar(hi, mx, -1.0, None, ALU.mult).then_inc(neghi_ok.sem, 1)
                            need(dve, neghi_ok, pair, q + 1)
                            dve.scalar_tensor_tensor(out=lo, in0=mx, scalar=-1.0, in1=hi, op0=ALU.mult,
                                                     op1=ALU.subtract).then_inc(negmax_ok.sem, 1)
                    for pair, a in stages(p, s, tail, late):
                        after_attention(pair, a)
                    if s in XT_SLOT and head:
                        c = XT_SLOT[s]
                        need(dve, xT_hi_ok, p + 1, c + 1)
                        dve.tensor_tensor(out=xT_lo[:, c, :], in0=ps_head[:, :],
                                          in1=xT_hi[:, c, :].bitcast(F32), op=ALU.subtract)\
                            .then_inc(xT_lo_ok.sem, 1)
                    if s in QK_SLOT and head:
                        c, i = QK_SLOT[s]
                        n = 2 * c + i + 1
                        need(dve, qk_hi_ok, p + 1, n)
                        need(dve, low_ok, p + 1, n - 2)
                        dve.scalar_tensor_tensor(out=rest[:, i, :], in0=ps_head[:, :], scalar=bqk[:, i, c:c + 1],
                                                 in1=parts[i][:, c, HI[i], :], op0=ALU.add, op1=ALU.subtract)\
                            .then_inc(rest_ok.sem, 1)
                        dve.tensor_copy(parts[i][:, c, HI_COPIES[i], :],
                                        parts[i][:, c, HI[i]:HI[i] + 1, :].to_broadcast([P, 2, TOK]))\
                            .then_inc(copies_ok.sem, 1)

            run(dve, iteration)

        @block.tensor
        def _(pe):
            def three_passes(dst, st_hi, st_lo, mv_hi, mv_lo, chunks):
                n = 0
                for c in range(chunks):
                    for a, m in ((st_hi, mv_hi), (st_hi, mv_lo), (st_lo, mv_hi)):
                        last = pe.matmul(dst, a(c), m(c), start=(n == 0), stop=(n == 3 * chunks - 1))
                        n += 1
                return last

            pe.wait_ge(cst, 8)
            pe.wait_ge(vcst, 4)
            pe.matmul(ps_av[:, 0:1], ones[:, :], wf_abs[:, :], start=True, stop=True).then_inc(prep_mm, 1)
            pe.wait_ge(w_in.sem, W_IN)

            def transpose_weights(i, src):
                dst = ps_tail[0] if i % 2 else ps_head
                for ci in range(EC):
                    for co in range(EC):
                        last = pe.transpose(dst[:, ci * E + co * P:ci * E + co * P + P],
                                            src[:, co, ci * P:(ci + 1) * P], ident[:, :])
                last.then_inc(prep_mm, 1)

            for i in range(4):
                if i >= 2:
                    pe.wait_ge(prep_lo, i - 1)
                transpose_weights(i, w_raw[:, i])
            pe.wait_ge(vcst, 12)
            pe.wait_ge(prep_lo, 4)
            transpose_weights(4, wf_q)
            n = 0
            for c in range(EC):
                for part in (wT_hi[3], wT_lo[3]):
                    pe.matmul(ps_av[:, 0:E], bv_bc[:, c, :], part[:, c, :].bitcast(F32), start=(n == 0), stop=False)
                    n += 1
            pe.matmul(ps_av[:, 0:E], ones[0:1, :], bp_row[:, :], start=False, stop=True).then_inc(prep_mm, 1)
            pe.wait_ge(prep_hi, 5)
            pe.wait_ge(prep_lo, 5)

            def after_attention(pair, a):
                if a in FFN_SLOT:
                    b = FFN_SLOT[a]
                    need(pe, h2T_lo_ok, pair, 2)
                    for t in range(T):
                        tok = slice((T * b + t) * P, (T * b + t + 1) * P)
                        n = 0
                        for c in range(EC):
                            for part in (h2T_hi, h2T_lo):
                                last = pe.matmul(ps_tail[b][:, t * E:(t + 1) * E], part[:, c, tok], wfT[:, c, :],
                                                 start=(n == 0), stop=(n == 2 * EC - 1))
                                n += 1
                    last.then_inc(mm_ffn.sem, 1)
                if a in HEADS_SLOT:
                    for k in HEADS_SLOT[a]:
                        b, t = k // T, k % T
                        if k == 0:
                            need(pe, y_ok, pair, 4)
                        if k < 2:
                            need(pe, z_ok, pair - 1, 5 + k)
                        else:
                            need(pe, yn_ok, pair, k - 1)
                        for q in range(QUADS):
                            last = pe.transpose(ps_tail[k % 2][:, q * P:(q + 1) * P],
                                                y_sb[:, q, b, t * P:(t + 1) * P], ident[:, :])
                        last.then_inc(mm_y.sem, 1)
                if a == YNT_SLOT:
                    need(pe, yn_ok, pair, 4)
                    for c in range(EC):
                        for k in range(KT):
                            last = pe.transpose(ps_tail[c][:, k * P:(k + 1) * P], yn[:, k, c * P:(c + 1) * P],
                                                ident[:, :])
                        last.then_inc(mm_ynT.sem, 1)
                if a in PROJ_SLOT:
                    b = PROJ_SLOT[a]
                    need(pe, ynT_lo_ok, pair, 2)
                    for t in range(T):
                        tok = slice((T * b + t) * P, (T * b + t + 1) * P)
                        last = three_passes(ps_tail[b][:, t * E:(t + 1) * E],
                                            lambda c: ynT_hi[:, c, tok], lambda c: ynT_lo[:, c, tok],
                                            lambda c: wT_hi[3][:, c, :], lambda c: wT_lo[3][:, c, :], EC)
                    last.then_inc(mm_proj.sem, 1)
                if a == CTXT_SLOT:
                    need(pe, ctx_landed, pair, 1)
                    need(pe, z_ok, pair, 1)
                    for b in range(PB):
                        for c in range(EC):
                            n = b * EC + c
                            last = pe.transpose(ps_tail[0][:, n * CP:n * CP + C],
                                                ctx_sb[:, b, c * P:(c + 1) * P], ident[0:C, 0:C])
                    last.then_inc(mm_ctxT.sem, 1)
                if a == H1T_SLOT:
                    need(pe, norm_ok, pair, 2)
                    need(pe, ctxT_ok, pair, 1)
                    for c in range(EC):
                        for k in range(KT):
                            last = pe.transpose(ps_tail[c][:, k * P:(k + 1) * P], h1[:, k, c * P:(c + 1) * P],
                                                ident[:, :])
                        last.then_inc(mm_h1T.sem, 1)
                if a == SCORE_SLOT:
                    need(pe, h1T_ok, pair, 2)
                    for k in range(KT):
                        for c in range(EC):
                            last = pe.matmul(ps_tail[0][:, k * CP:k * CP + C], h1T[:, c, k * P:(k + 1) * P],
                                             ctxT[:, (k // T) * EC + c, 0:C], start=(c == 0), stop=(c == EC - 1))
                    last.then_inc(mm_sc.sem, 1)
                if a == PT_SLOT:
                    need(pe, p2_ok, pair, 1)
                    for k in range(KT):
                        last = pe.transpose(ps_tail[1][0:C, k * P:(k + 1) * P], p2[:, k, :], ident[:, :])
                    last.then_inc(mm_pT.sem, 1)
                if a == XAV_SLOT:
                    need(pe, p2T_ok, pair, 1)
                    for b in range(PB):
                        for t in range(T):
                            k = T * b + t
                            last = pe.matmul(ps_tail[b][:, t * E:(t + 1) * E], p2T[:, k * P:(k + 1) * P],
                                             ctx_sb[:, b, :], start=True, stop=True)
                        last.then_inc(mm_xav.sem, 1)
                if a == H2T_SLOT:
                    need(pe, norm_ok, pair, 4)
                    for c in range(EC):
                        for k in range(KT):
                            last = pe.transpose(ps_tail[c][:, k * P:(k + 1) * P], h2[:, k, c * P:(c + 1) * P],
                                                ident[:, :])
                        last.then_inc(mm_h2T.sem, 1)

            def iteration(p, load=False, head=False, main=False, tail=False, late=False):
                for s in range(SLOTS):
                    if main:
                        q, b, u = s // 6, s // 3 % 2, s % 3
                        if s % 6 == 0:
                            need(pe, mrow_in[q], p, 1)
                        need(pe, exp_ok, p, s - 1)
                        t0 = b * S
                        for j in (range(4) if u == 2 else range(2 * u, 2 * u + 2)):
                            h = 4 * q + j
                            if u == 2:
                                keys, queries, at = slice(t0 + P, t0 + S), slice(t0 + P, t0 + S), P * j
                            else:
                                keys, queries, at = slice(t0, t0 + P), slice(t0, t0 + S), S * (j % 2)
                            last = pe.matmul(ps_st[s % 2][:, at:at + queries.stop - queries.start],
                                             stack[1][0:KROWS + 2, h, keys], stack[0][0:KROWS + 2, h, queries],
                                             start=True, stop=True)
                        last.then_inc(mm_st.sem, 1)
                    unit = max_unit(p, s, main, head)
                    if unit:
                        pair, n = unit
                        q, b, u = n // 6, n // 3 % 2, n % 3
                        if n % 6 == 0:
                            need(pe, stack_in[q], pair, 8)
                        need(pe, max_ok, pair, n - 1)
                        t0 = b * S
                        queries = slice(t0, t0 + P) if u == 0 else slice(t0 + P, t0 + S)
                        keys = slice(t0 + P, t0 + S) if u == 2 else slice(t0, t0 + P)
                        if u != 1:
                            pe.matmul(ps_max[n % 2][:, :], ident_b[:, :],
                                      causal_b[:, :, :].rearrange("p j c -> p (j c)"), start=True, stop=False)
                        for j in range(4):
                            h = 4 * q + j
                            last = pe.matmul(ps_max[n % 2][:, P * j:P * j + P], stack[0][0:KROWS, h, queries],
                                             stack[1][0:KROWS, h, keys], start=(u == 1), stop=(u == 1 or j == 3))
                        last.then_inc(mm_max.sem, 1)
                    av = {5: (0, 0), 8: (0, 1), 11: (1, 0), 14: (1, 1), 17: (2, 0), 20: (2, 1), 23: (3, 0),
                          2: (3, 1)}.get(s)
                    if av and (tail if s == 2 else main):
                        q, b = av
                        pair = p - (s == 2)
                        need(pe, sel_ok, pair, 6 * q + 3 * b + 3)
                        if q == 0:
                            need(pe, v_ok, pair, b + 1)
                        if b == 0:
                            need(pe, y_ok, pair, q)
                            if q < 3 or head:
                                need(pe, mT_ok, pair, q + 2)
                        for kb in range(T):
                            for j in range(4):
                                if kb == 0:
                                    pr = probs[:, q % 2, 3 * b + j // 2, S * (j % 2):S * (j % 2) + S]
                                else:
                                    pr = probs[:, q % 2, 3 * b + 2, P * j:P * j + P]
                                last = pe.matmul(ps_av[HW * j:HW * j + HW, b * S + kb * P:b * S + S],
                                                 v_ext[:, T * b + kb, 4 * q + j, :], pr,
                                                 start=(kb == 0), stop=(kb == 1), skip_group_check=True,
                                                 tile_position=(0, HW * j))
                        last.then_inc(mm_av.sem, 1)
                    if s in MT_SLOT and (head if s == 21 else main):
                        q, pair = MT_SLOT[s], p + (s == 21)
                        need(pe, negmax_ok, pair, q + 1)
                        need(pe, y_ok, pair, q - 1)
                        for b in range(PB):
                            for t in range(T):
                                at = (T * b + t) * P
                                last = pe.transpose(ps_av[:, :].bitcast(BF16)[0:8, at:at + P],
                                                    negmax[:, b, t, :, :].rearrange("p i j -> p (i j)"), ident_b[:, :])
                        last.then_inc(mm_mT.sem, 1)
                    for pair, a in stages(p, s, tail, late):
                        after_attention(pair, a)
                    if s in XT_SLOT and head:
                        c = XT_SLOT[s]
                        if c == 0:
                            need(pe, x_in, p + 1, 1)
                            need(pe, v_ok, p, 2)
                        else:
                            need(pe, xT_lo_ok, p + 1, 1)
                        for k in range(KT):
                            last = pe.transpose(ps_head[:, k * P:(k + 1) * P], xt[:, k, c * P:(c + 1) * P],
                                                ident[:, :])
                        last.then_inc(mm_xT.sem, 1)
                    if s in QK_SLOT and head:
                        c, i = QK_SLOT[s]
                        n = 2 * c + i + 1
                        if n == 1:
                            need(pe, xT_lo_ok, p + 1, 2)
                        else:
                            need(pe, rest_ok, p + 1, n - 1)
                        out_c = slice(c * P, (c + 1) * P)
                        three_passes(ps_head[:, :],
                                     lambda k: wT_hi[i][:, k, out_c], lambda k: wT_lo[i][:, k, out_c],
                                     lambda k: xT_hi[:, k, :], lambda k: xT_lo[:, k, :], EC)\
                            .then_inc(mm_qk.sem, 1)
                    if s in V_SLOT and main:
                        b = V_SLOT[s]
                        if b == 0:
                            need(pe, rest_ok, p, 4)
                        else:
                            need(pe, v_ok, p, 1)
                        for t in range(T):
                            tok = slice((T * b + t) * P, (T * b + t + 1) * P)
                            last = three_passes(ps_head[:, t * E:(t + 1) * E],
                                                lambda c: xT_hi[:, c, tok], lambda c: xT_lo[:, c, tok],
                                                lambda c: wT_hi[2][:, c, :], lambda c: wT_lo[2][:, c, :], EC)
                        last.then_inc(mm_v.sem, 1)

            run(pe, iteration)


_INS = ["x", "ctx_1024", "L0_attn_Wq", "L0_attn_bq", "L0_attn_Wk", "L0_attn_bk", "L0_attn_Wv", "L0_attn_bv",
        "L0_attn_Wp", "L0_attn_bp", "L0_ffn_weight"]


def kernel(**inputs):
    import numpy as _np
    import concourse.bacc as _bacc
    from concourse import mybir as _mybir
    from concourse.bass_utils import run_bass_kernel_spmd as _run

    nc = _bacc.Bacc("TRN2", target_bir_lowering=False, num_devices=1)
    arrays, args = {}, []
    for name in _INS:
        a = _np.ascontiguousarray(inputs[name])
        arrays[f"in_{name}"] = a
        args.append(nc.dram_tensor(f"in_{name}", a.shape, _mybir.dt.from_np(a.dtype), kind="ExternalInput").ap())
    shape = inputs["x"].shape
    args.append(nc.dram_tensor("out_0", shape, _mybir.dt.float32, kind="ExternalOutput").ap())
    decoder_layer(nc, *args)
    r = _run(nc, [arrays], core_ids=[0])
    return r.results[0]["out_0"]
```

```python
from contextlib import ExitStack

import concourse.bass as bass
from concourse import mybir

F32 = mybir.dt.float32
F32R = mybir.dt.float32r
BF16 = mybir.dt.bfloat16
ALU = mybir.AluOpType
ACT = mybir.ActivationFunctionType
AX = mybir.AxisListType

P = 128
HEADS = 16
DH = 16
QUADS = 4
PB = 2
SLOTS = 24
HW = 32
NPARTS = 6
KROWS = NPARTS * DH
LEAD = 10
NEG = -1.0e30
EPS = 1e-5


def decoder_layer(nc, x, ctx_in, wq, bq, wk, bk, wv, bv, wp, bp, wf, out):
    B, S, E = x.shape
    C = ctx_in.shape[1]
    NP = B // PB
    T = S // P
    KT = PB * T
    EC = E // P
    TOK = PB * S
    CP = 80
    SCALE = float(DH) ** -0.5
    assert (T, EC, KT, TOK, HEADS * DH) == (2, 2, 4, 512, E) and 6 * QUADS == SLOTS and NP >= 5

    x_tiles = x.rearrange("b (t p) d -> p (b t) d", p=P)
    out_tiles = out.rearrange("b (t p) d -> p (b t) d", p=P)
    ctx_rows = ctx_in.rearrange("b k d -> k b d")

    with ExitStack() as ctx:
        def sb(name, shape, dt=F32):
            return ctx.enter_context(nc.sbuf_tensor(name, shape, dt))

        def bank(name):
            return ctx.enter_context(nc.psum_tensor(name, [P, 512], F32))

        class Signal:

            def __init__(self, name, per, step=1):
                self.sem = ctx.enter_context(nc.semaphore(name))
                self.per, self.step = per, step

            def value(self, pair, k):
                return pair * (self.per * self.step) + k * self.step

        def need(eng, signal, pair, k):
            v = signal.value(pair, k)
            if isinstance(v, int) and v <= 0:
                return
            eng.wait_ge(signal.sem, v)

        def need_apart(eng, signal, pair, k):
            v = signal.value(pair, k)
            if isinstance(v, int):
                return need(eng, signal, pair, k)
            v = eng.to_reg(v)
            eng.wait_ge(cst, CONSTANTS)
            eng.wait_ge(signal.sem, v)

        ps_av, ps_head = bank("ps_av"), bank("ps_head")
        ps_tail, ps_max, ps_st = ([bank(f"{n}{i}") for i in range(2)] for n in ("ps_tail", "ps_max", "ps_st"))

        ident = sb("ident", [P, P])
        ident_b = sb("ident_b", [P, P], BF16)
        causal_b = sb("causal_b", [P, 4, P], BF16)
        xmask = sb("xmask", [P, KT, C])
        neg_half = sb("neg_half", [P, KT])
        ones = sb("ones", [P, P])
        zeros = sb("zeros", [P, PB * T * 4])
        w_raw = sb("w_raw", [P, 5, EC, E])
        wT_hi = [sb(f"wT_hi{i}", [P, EC, E], F32R) for i in range(4)]
        wT_lo = [sb(f"wT_lo{i}", [P, EC, E], F32R) for i in range(4)]
        wfT = sb("wfT", [P, EC, E], F32R)
        bqk = sb("bqk", [P, 2, EC])
        bv_col = sb("bv_col", [P, EC])
        bv_bc = sb("bv_bc", [P, EC, P])
        bp_row = sb("bp_row", [1, E])
        bias_bc = sb("bias_bc", [P, E])
        wf_abs = sb("wf_abs", [P, 1])
        fscale = sb("fscale", [P, 1])
        wf_half = sb("wf_half", [P, 2])

        xt = sb("xt", [P, KT, E])
        xT_hi = sb("xT_hi", [P, EC, TOK], F32R)
        xT_lo = sb("xT_lo", [P, EC, TOK], F32R)
        parts = [sb(f"parts{i}", [P, EC, NPARTS, TOK], BF16) for i in range(2)]
        rest = sb("rest", [P, 2, TOK])
        stack = [sb(f"stack{i}", [P, HEADS, TOK], BF16) for i in range(2)]

        v_ext = sb("v_ext", [P, KT, HEADS, HW])
        rowmax = sb("rowmax", [P, 2, PB, T, 4])
        rowmax2 = sb("rowmax2", [P, 2, PB, 4])
        negmax = sb("negmax", [P, PB, T, 2, 4], BF16)
        negmax_t = sb("negmax_t", [8, TOK], BF16)
        probs = sb("probs", [P, 2, 6, 512])

        xres = sb("xres", [P, KT, E])
        ctx_sb = sb("ctx_sb", [C, PB, E])
        ctxT = sb("ctxT", [P, PB * EC, CP])
        y_sb = sb("y_sb", [P, QUADS, PB, S])
        rden = sb("rden", [P, KT, HEADS])
        yn = sb("yn", [P, KT, E])
        ynT_hi = sb("ynT_hi", [P, EC, TOK], F32R)
        ynT_lo = sb("ynT_lo", [P, EC, TOK], F32R)
        zs = [sb(f"z{i}", [P, KT, E]) for i in range(2)]
        bnst = sb("bnst", [P, KT, 6])
        mv = sb("mv", [P, KT, 2])
        vareps = sb("vareps", [P, KT])
        negmean = sb("negmean", [P, KT])
        rstd = sb("rstd", [P, KT])
        shift = sb("shift", [P, KT])
        h1 = sb("h1", [P, KT, E])
        h1T = sb("h1T", [P, EC, TOK])
        sc = sb("sc", [P, KT, C])
        nmx = sb("nmx", [P, KT])
        p2 = sb("p2", [P, KT, C])
        ssum = sb("ssum", [P, KT])
        rsum = sb("rsum", [P, KT])
        p2T = sb("p2T", [C, TOK])
        h2 = sb("h2", [P, KT, E])
        h2T_hi = sb("h2T_hi", [P, EC, TOK], F32R)
        h2T_lo = sb("h2T_lo", [P, EC, TOK], F32R)
        o_sb = sb("o_sb", [P, KT, E])

        wf_q, wf_n = h1[:, 0:EC, :], h1[:, EC:2 * EC, :]

        W_IN = 16 * 9
        w_in = Signal("w_in", 1, W_IN)
        x_in = Signal("x_in", 1, 16)
        xres_in = Signal("xres_in", 1, 16)
        ctx_landed = Signal("ctx_landed", 1, 16)
        stack_in = [[Signal(f"{n}_stack_in{q}", 4, 16) for n in "qk"] for q in range(QUADS)]
        mrow_in = [Signal(f"mrow_in{q}", 1, 16) for q in range(QUADS)]
        out_done = [Signal(f"out_done{b}", 1, 16) for b in range(PB)]
        mm_xT, mm_qk, mm_v = Signal("mm_xT", 2), Signal("mm_qk", 4), Signal("mm_v", 2)
        mm_mT, mm_ctxT = Signal("mm_mT", 4), Signal("mm_ctxT", 1)
        mm_max, mm_st, mm_av = Signal("mm_max", SLOTS), Signal("mm_st", SLOTS), Signal("mm_av", 8)
        mm_y, mm_ynT, mm_proj = Signal("mm_y", 4), Signal("mm_ynT", 2), Signal("mm_proj", 2)
        mm_h1T, mm_sc, mm_pT = Signal("mm_h1T", 2), Signal("mm_sc", 1), Signal("mm_pT", 1)
        mm_xav, mm_h2T, mm_ffn = Signal("mm_xav", 2), Signal("mm_h2T", 2), Signal("mm_ffn", 2)
        xT_hi_ok, qk_hi_ok, v_ok = Signal("xT_hi_ok", 2), Signal("qk_hi_ok", 4), Signal("v_ok", 2)
        ctxT_ok, exp_ok, y_ok = Signal("ctxT_ok", 1), Signal("exp_ok", SLOTS), Signal("y_ok", 4)
        ynT_hi_ok, h1T_ok = Signal("ynT_hi_ok", 2), Signal("h1T_ok", 2)
        p2_ok, p2T_ok, h2T_hi_ok = Signal("p2_ok", 1), Signal("p2T_ok", 1), Signal("h2T_hi_ok", 2)
        mid_ok, mT_ok = Signal("mid_ok", 4), Signal("mT_ok", 4)
        xT_lo_ok, rest_ok, copies_ok = Signal("xT_lo_ok", 2), Signal("rest_ok", 4), Signal("copies_ok", 4)
        max_ok, max2_ok = Signal("max_ok", SLOTS), Signal("max2_ok", 4)
        rden_ok, yn_ok, ynT_lo_ok = Signal("rden_ok", 4), Signal("yn_ok", 4), Signal("ynT_lo_ok", 2)
        z_ok, stats_ok, mv_ok = Signal("z_ok", 6), Signal("stats_ok", 3), Signal("mv_ok", 3)
        var_ok, norm_ok = Signal("var_ok", 3), Signal("norm_ok", 6)
        sc_ok, nmx_ok, rsum_ok = Signal("sc_ok", 1), Signal("nmx_ok", 1), Signal("rsum_ok", 1)
        h2T_lo_ok = Signal("h2T_lo_ok", 2)
        neghi_ok, negmax_ok = Signal("neghi_ok", 4), Signal("negmax_ok", 4)
        sel_ok, low_ok, xres_ok = Signal("sel_ok", SLOTS), Signal("low_ok", 4), Signal("xres_ok", 1)
        rstd_ok, shift_ok = Signal("rstd_ok", 3), Signal("shift_ok", 3)
        cst = ctx.enter_context(nc.semaphore("cst"))
        CONSTANTS = 10 + KT
        vcst = ctx.enter_context(nc.semaphore("vcst"))
        prep_mm = ctx.enter_context(nc.semaphore("prep_mm"))
        prep_hi = ctx.enter_context(nc.semaphore("prep_hi"))
        prep_lo = ctx.enter_context(nc.semaphore("prep_lo"))

        block = ctx.enter_context(nc.Block())

        def run(eng, iteration):
            iteration(-1, load=True, head=True)
            iteration(0, load=True, head=True, main=True)
            iteration(1, load=True, head=True, main=True, tail=True)
            iteration(2, load=True, head=True, main=True, tail=True, late=True)
            with eng.Fori(3, NP - 2) as p:
                iteration(p, load=True, head=True, main=True, tail=True, late=True)
            iteration(NP - 2, head=True, main=True, tail=True, late=True)
            iteration(NP - 1, main=True, tail=True, late=True)
            iteration(NP, tail=True, late=True)
            iteration(NP + 1, late=True)

        def max_unit(p, s, main, head):
            if s + LEAD < SLOTS:
                return (p, s + LEAD) if main else None
            return (p + 1, s + LEAD - SLOTS) if head else None

        MT_SLOT = {21: 0, 3: 1, 9: 2, 15: 3}
        STACK_SLOT = {0: ((3, 1),), 3: ((3, 0),), 9: ((0, 0),), 11: ((0, 1),),
                      14: ((1, 0),), 16: ((1, 1),), 19: ((2, 0),), 21: ((2, 1),)}
        X_SLOT, RES_SLOT, BIAS_SLOT = 4, 2, 3
        XT_SLOT, XT_HI_SLOT, XT_LO_SLOT = {3: 0, 4: 1}, {3.5: 0, 4: 1}, {3.5: 0, 4: 1}
        QK_SLOT = {5: (0, 0), 7.5: (0, 1), 14.5: (1, 0), 16: (1, 1)}
        QK_HI_SLOT = {5: (0, 0), 7.5: (0, 1), 14.5: (1, 0), 16: (1, 1)}
        QK_REST_SLOT = {5.5: (0, 0), 8: (0, 1), 14.5: (1, 0), 16.5: (1, 1)}
        QK_MID_SLOT = {6.5: (0, 0), 8.5: (0, 1), 16: (1, 0), 18.5: (1, 1)}
        QK_LOW_SLOT = {7: (0, 0), 10: (0, 1), 17: (1, 0), 20: (1, 1)}
        V_SLOT, V_READ_SLOT = {0: 0, 1.5: 1}, {0: 0, 2.5: 1}
        HEADS_SLOT, DIVIDE_SLOT = {6: (0, 1), 8: (2, 3)}, {6.5: (0, 1), 8.5: (2, 3)}
        YNT_SLOT, YNT_HI_SLOT, YNT_LO_SLOT = 10.5, 10.5, 10.5
        PROJ_SLOT, PROJ_READ_SLOT = {12: 0, 13: 1}, {12: 0, 13: 1}
        CTXT_SLOT, CTXT_READ_SLOT = 13, 13.5
        STATS_SLOT, POW_SLOT = {13.5: 0, 22: 1, 28.5: 2}, {14: 0, 24: 1, 29: 2}
        NORM_SLOT = {14: (0, 0), 15: (0, 1), 24.5: (1, 0), 25: (1, 1), 30.5: (2, 0), 36.5: (2, 1)}
        H1T_SLOT, H1T_READ_SLOT = 16.5, 16.5
        SCORE_SLOT, SCORE_MAX_SLOT, SOFTMAX_SLOT = 18, 18, 19.5
        PT_SLOT, PT_READ_SLOT, RSUM_SLOT = 20, 20.5, 21
        XAV_SLOT, XAV_READ_SLOT = 22, {22: (0, 1)}
        H2T_SLOT, H2T_HI_SLOT, H2T_LO_SLOT = 26.5, 26.5, 26.5
        FFN_SLOT, FFN_READ_SLOT = {28: 0, 28.5: 1}, {28: 0, 28.5: 1}
        STORE_SLOT = 39

        def stages(p, s, tail, late):
            return [(p - 2, s + SLOTS)] * late + [(p - 1, s)] * tail

        HI, HI_COPIES = (0, 2), (slice(1, 3), slice(3, 5))
        MID, MIDS, LOW = (3, 0), (slice(3, 6, 2), slice(0, 6, 5)), (4, 1)

        @block.sync
        def _(sp):
            sp.dma_start(xt[:, :, :], x_tiles[:, 0:KT, :]).then_inc(x_in.sem, 16)
            for i, w in enumerate((wq, wk, wv, wp, wf)):
                sp.dma_start(w_raw[:, i], w.rearrange("(c p) e -> p c e", p=P)).then_inc(w_in.sem, 16)
            with nc.allow_non_contiguous_dma(reason="biases by partition"):
                for i, b in enumerate((bq, bk)):
                    sp.dma_start(bqk[:, i, :], b.rearrange("(c p) -> p c", p=P)).then_inc(w_in.sem, 16)
                sp.dma_start(bv_col[:, :], bv.rearrange("(c p) -> p c", p=P)).then_inc(w_in.sem, 16)
            sp.dma_start(bp_row[:, :], bp.rearrange("(a e) -> a e", a=1)).then_inc(w_in.sem, 16)

            def copy_stack(q, i, pair):
                c = q // 2
                need_apart(sp, copies_ok, pair, 2 * c + i + 1)
                need_apart(sp, low_ok, pair, 2 * c + i + 1)
                need_apart(sp, mm_st, pair - 1, 6 * q + 6)
                for j in range(4):
                    h = 4 * q + j
                    r = h % 8
                    sp.dma_start(stack[i][0:KROWS, h, :], parts[i][DH * r:DH * r + DH, c, :, :])\
                        .then_inc(stack_in[q][i].sem, 16)

            def iteration(p, load=False, head=False, main=False, tail=False, late=False):
                for s in range(SLOTS):
                    if s == X_SLOT and load:
                        need_apart(sp, mm_xT, p + 1, 2)
                        sp.dma_start(xt[:, :, :], x_tiles[:, bass.ds((p + 2) * KT, KT), :])\
                            .then_inc(x_in.sem, 16)
                    if s == RES_SLOT and tail:
                        need_apart(sp, z_ok, p - 2, 2)
                        sp.dma_start(xres[:, :, :], x_tiles[:, bass.ds((p - 1) * KT, KT), :])\
                            .then_inc(xres_in.sem, 16)
                        need_apart(sp, mm_xav, p - 2, 2)
                        sp.dma_start(ctx_sb[:, :, :], ctx_rows[:, bass.ds((p - 1) * PB, PB), :])\
                            .then_inc(ctx_landed.sem, 16)
                    if s in MT_SLOT and (main if MT_SLOT[s] else head):
                        q, pair = MT_SLOT[s], p + (MT_SLOT[s] == 0)
                        need_apart(sp, mT_ok, pair, q + 1)
                        sp.dma_start(stack[0][KROWS:KROWS + 2, 4 * q:4 * q + 4, :], negmax_t[:, :])\
                            .then_inc(mrow_in[q].sem, 16)
                    for q, i in STACK_SLOT.get(s, ()):
                        if q == 3 and main:
                            copy_stack(q, i, p)
                        if q < 3 and head:
                            copy_stack(q, i, p + 1)
                    for pair, a in stages(p, s, tail, late):
                        if a == STORE_SLOT:
                            for b in range(PB):
                                need_apart(sp, norm_ok, pair, 5 + b)
                                sp.dma_start(out_tiles[:, bass.ds(pair * KT + T * b, T), :],
                                             o_sb[:, T * b:T * b + T, :]).then_inc(out_done[b].sem, 16)

            run(sp, iteration)
            for b in range(PB):
                sp.wait_ge(out_done[b].sem, 16 * NP)

        @block.gpsimd
        def _(pool):
            pool.memset(ident[:, :], 0.0).then_inc(cst, 1)
            pool.memset(ident_b[:, :], 0.0).then_inc(cst, 1)
            pool.memset(causal_b[:, :, :], 0.0).then_inc(cst, 1)
            pool.memset(xmask[:, :, :], 0.0).then_inc(cst, 1)
            pool.memset(neg_half[:, :], -0.5).then_inc(cst, 1)
            pool.memset(ones[:, :], 1.0).then_inc(cst, 1)
            pool.memset(zeros[:, :], 0.0).then_inc(cst, 1)
            pool.wait_ge(cst, 7)
            for m in (ident, ident_b):
                pool.affine_select(out=m[:, :], in_=m[:, :], compare_op=ALU.not_equal, fill=1.0, base=0,
                                   pattern=[[-1, P]], channel_multiplier=1).then_inc(cst, 1)
            pool.affine_select(out=causal_b[:, :, :], in_=causal_b[:, :, :], compare_op=ALU.is_ge, fill=NEG,
                               base=0, pattern=[[0, 4], [-1, P]], channel_multiplier=1).then_inc(cst, 1)
            for b in range(PB):
                for t in range(T):
                    k = T * b + t
                    pool.affine_select(out=xmask[:, k, :], in_=xmask[:, k, :], compare_op=ALU.is_ge,
                                       fill=-1.0e9, base=P * t, pattern=[[-1, C]],
                                       channel_multiplier=1).then_inc(cst, 1)

            def iteration(p, load=False, head=False, main=False, tail=False, late=False):
                for s in range(SLOTS):
                    if main:
                        q, u = s // 6, s % 3
                        buf = probs[:, q % 2, s % 6, :]
                        n, w = (4, P) if u == 2 else (2, S)
                        part = buf.rearrange("p (j c) -> p j c", c=w)[:, :, 0:P]
                        need_apart(pool, exp_ok, p, s + 1)
                        pool.affine_select(out=part, in_=part, compare_op=ALU.is_ge, fill=0.0, base=0,
                                           pattern=[[0, n], [1, P]], channel_multiplier=-1)\
                            .then_inc(sel_ok.sem, 1)
                    unit = max_unit(p, s, main, head)
                    if unit and unit[1] % 6 == 5:
                        pair, n = unit
                        q = n // 6
                        m = rowmax[:, q % 2]
                        need(pool, max2_ok, pair, q + 1)
                        need(pool, mm_mT, pair, q)
                        mx = m.rearrange("p b t j -> p (b t) j")
                        hi, lo = (negmax[:, :, :, i, :].rearrange("p b t j -> p (b t) j") for i in range(2))
                        pool.tensor_tensor(out=hi, in0=mx, in1=zeros[:, :].rearrange("p (k j) -> p k j", j=4),
                                           op=ALU.add).then_inc(neghi_ok.sem, 1)
                        need(pool, neghi_ok, pair, q + 1)
                        pool.tensor_tensor(out=lo, in0=mx, in1=hi, op=ALU.subtract).then_inc(negmax_ok.sem, 1)
                    if s == BIAS_SLOT and tail:
                        need(pool, xres_in, p - 1, 1)
                        if isinstance(p, int) and p == 1:
                            pool.wait_ge(prep_lo, 5)
                        pool.tensor_tensor(out=xres[:, :, :], in0=xres[:, :, :],
                                           in1=bias_bc[:, :].unsqueeze(1).to_broadcast([P, KT, E]),
                                           op=ALU.add).then_inc(xres_ok.sem, 1)
                    if s in QK_LOW_SLOT and head:
                        c, i = QK_LOW_SLOT[s]
                        n = 2 * c + i + 1
                        need(pool, mid_ok, p + 1, n)
                        pool.tensor_tensor(out=parts[i][:, c, LOW[i], :], in0=rest[:, i, :],
                                           in1=parts[i][:, c, MID[i], :], op=ALU.subtract)\
                            .then_inc(low_ok.sem, 1)
                    for pair, a in stages(p, s, tail, late):
                        if a in POW_SLOT:
                            ln = POW_SLOT[a]
                            need(pool, var_ok, pair, ln + 1)
                            pool.tensor_tensor(out=rstd[:, :], in0=vareps[:, :], in1=neg_half[:, :],
                                               op=ALU.pow).then_inc(rstd_ok.sem, 1)
                            need(pool, rstd_ok, pair, ln + 1)
                            pool.tensor_tensor(out=shift[:, :], in0=negmean[:, :], in1=rstd[:, :],
                                               op=ALU.mult).then_inc(shift_ok.sem, 1)

            run(pool, iteration)

        @block.scalar
        def _(act):
            for i in range(5):
                act.wait_ge(prep_mm, i + 2)
                dst = wfT if i == 4 else wT_hi[i]
                act.activation(dst[:, :, :].rearrange("p c e -> p (c e)"), ps_tail[0][:, :] if i % 2 else ps_head[:, :],
                               ACT.Copy).then_inc(prep_hi, 1)

            def normalize(pair, ln, b, dst):
                need(act, shift_ok, pair, ln + 1)
                for k in (T * b, T * b + 1):
                    last = act.activation(dst[:, k, :], zs[ln % 2][:, k, :], ACT.Identity, bias=shift[:, k:k + 1],
                                          scale=rstd[:, k:k + 1])
                last.then_inc(norm_ok.sem, 1)

            def after_attention(pair, a):
                if a in NORM_SLOT:
                    ln, b = NORM_SLOT[a]
                    if ln == 2:
                        need(act, out_done[b], pair - 1, 1)
                    normalize(pair, ln, b, (h1, h2, o_sb)[ln])
                if a == YNT_HI_SLOT:
                    for c in range(EC):
                        need(act, mm_ynT, pair, c + 1)
                        act.activation(ynT_hi[:, c, :], ps_tail[c][:, :], ACT.Copy).then_inc(ynT_hi_ok.sem, 1)
                if a == CTXT_READ_SLOT:
                    need(act, mm_ctxT, pair, 1)
                    act.activation(ctxT[:, :, 0:C],
                                   ps_tail[0][:, 0:PB * EC * CP].rearrange("p (n c) -> p n c", c=CP)[:, :, 0:C],
                                   ACT.Copy).then_inc(ctxT_ok.sem, 1)
                if a == H1T_READ_SLOT:
                    for c in range(EC):
                        need(act, mm_h1T, pair, c + 1)
                        act.activation(h1T[:, c, :], ps_tail[c][:, :], ACT.Copy).then_inc(h1T_ok.sem, 1)
                if a == SOFTMAX_SLOT:
                    need(act, nmx_ok, pair, 1)
                    need(act, rsum_ok, pair - 1, 1)
                    for k in range(KT):
                        last = act.activation(p2[:, k, :], sc[:, k, :], ACT.Exp, bias=nmx[:, k:k + 1],
                                              accum_out=ssum[:, k:k + 1])
                    last.then_inc(p2_ok.sem, 1)
                if a == PT_READ_SLOT:
                    need(act, mm_pT, pair, 1)
                    act.activation(p2T[:, :], ps_tail[1][0:C, :], ACT.Copy).then_inc(p2T_ok.sem, 1)
                if a == H2T_HI_SLOT:
                    for c in range(EC):
                        need(act, mm_h2T, pair, c + 1)
                        act.activation(h2T_hi[:, c, :], ps_tail[c][:, :], ACT.Copy).then_inc(h2T_hi_ok.sem, 1)

            def iteration(p, load=False, head=False, main=False, tail=False, late=False):
                for s in range(SLOTS):
                    if main:
                        q = s // 6
                        need(act, mm_st, p, s + 1)
                        need(act, mm_av, p, 2 * q - 2)
                        act.activation(probs[:, q % 2, s % 6, :], ps_st[s % 2][:, :], ACT.Exp,
                                       scale=SCALE).then_inc(exp_ok.sem, 1)
                    yq = {8: 0, 14: 1, 20: 2, 2: 3}.get(s)
                    if yq is not None and (tail if yq == 3 else main):
                        pair = p - (yq == 3)
                        need(act, mm_av, pair, 2 * yq + 2)
                        need(act, mm_y, pair - 1, 4)
                        act.activation(y_sb[:, yq, :, :].rearrange("p b s -> p (b s)"), ps_av[:, :],
                                       ACT.Copy).then_inc(y_ok.sem, 1)
                    if s in MT_SLOT and (main if MT_SLOT[s] else head):
                        q, pair = MT_SLOT[s], p + (MT_SLOT[s] == 0)
                        need(act, mm_mT, pair, q + 1)
                        need(act, mrow_in[(q - 1) % 4], pair - (q == 0), 1)
                        act.activation(negmax_t[:, :], ps_av[:, :].bitcast(BF16)[0:8, 0:TOK], ACT.Copy)\
                            .then_inc(mT_ok.sem, 1)
                    for t in (s, s + 0.5):
                        if t in QK_MID_SLOT and head:
                            c, i = QK_MID_SLOT[t]
                            n = 2 * c + i + 1
                            need(act, rest_ok, p + 1, n)
                            act.activation(parts[i][:, c, MIDS[i], :], rest[:, i:i + 1, :].to_broadcast([P, 2, TOK]),
                                           ACT.Copy).then_inc(mid_ok.sem, 1)
                        for pair, a in stages(p, t, tail, late):
                            after_attention(pair, a)
                        if t in XT_HI_SLOT and head:
                            c = XT_HI_SLOT[t]
                            need(act, mm_xT, p + 1, c + 1)
                            act.activation(xT_hi[:, c, :], ps_head[:, :], ACT.Copy).then_inc(xT_hi_ok.sem, 1)
                        if t in QK_HI_SLOT and head:
                            c, i = QK_HI_SLOT[t]
                            n = 2 * c + i + 1
                            need(act, mm_qk, p + 1, n)
                            for q in (2 * c, 2 * c + 1):
                                need(act, stack_in[q][i], p, 4)
                            act.activation(parts[i][:, c, HI[i], :], ps_head[:, :], ACT.Identity,
                                           bias=bqk[:, i, c:c + 1]).then_inc(qk_hi_ok.sem, 1)
                        if t in V_READ_SLOT and main:
                            b = V_READ_SLOT[t]
                            need(act, mm_v, p, b + 1)
                            need(act, mm_av, p - 1, 7 + b)
                            act.activation(v_ext[:, T * b:T * b + T, :, 0:DH].rearrange("p t h d -> p (t h) d"),
                                           ps_head[:, :].rearrange("p (n d) -> p n d", d=DH),
                                           ACT.Copy).then_inc(v_ok.sem, 1)

            run(act, iteration)

        @block.vector
        def _(dve):
            steps = [0]

            def step(ins):
                steps[0] += 1
                ins.then_inc(vcst, 1)
                dve.wait_ge(vcst, steps[0])

            dve.memset(v_ext[:, :, :, :], 0.0).then_inc(vcst, 1)
            dve.memset(stack[1][KROWS:KROWS + 2, :, :], 1.0).then_inc(vcst, 1)
            steps[0] = 2
            dve.wait_ge(vcst, 2)
            step(dve.memset(v_ext[:, :, :, DH:DH + 1], 1.0))
            dve.wait_ge(w_in.sem, W_IN)
            step(dve.tensor_reduce(wf_abs[:, :], w_raw[:, 4], axis=AX.XY, op=ALU.add,
                                   apply_absolute_value=True))
            dve.wait_ge(prep_mm, 1)
            step(dve.tensor_scalar(fscale[:, :], ps_av[:, 0:1], 1.0 / (E * E), EPS, ALU.mult, ALU.max))
            for i, half in enumerate((0.5, -0.5)):
                step(dve.tensor_scalar(wf_half[:, i:i + 1], fscale[:, :], half, None, ALU.mult))
            step(dve.tensor_scalar(wf_q, w_raw[:, 4], wf_half[:, 0:1], None, ALU.is_gt))
            step(dve.tensor_scalar(wf_n, w_raw[:, 4], wf_half[:, 1:2], None, ALU.is_lt))
            step(dve.tensor_tensor(out=wf_q, in0=wf_q, in1=wf_n, op=ALU.subtract))
            for c in range(EC):
                step(dve.tensor_scalar(bv_bc[:, c, :], ones[:, :], bv_col[:, c:c + 1], None, ALU.mult))
            for i in range(4):
                dve.wait_ge(prep_hi, i + 1)
                dve.tensor_tensor(out=wT_lo[i][:, :, :].rearrange("p c e -> p (c e)"),
                                  in0=ps_tail[0][:, :] if i % 2 else ps_head[:, :],
                                  in1=wT_hi[i][:, :, :].rearrange("p c e -> p (c e)").bitcast(F32),
                                  op=ALU.subtract).then_inc(prep_lo, 1)
            dve.wait_ge(prep_mm, 7)
            dve.tensor_copy(bias_bc[:, :], ps_av[:, 0:E]).then_inc(prep_lo, 1)

            def statistics(pair, ln):
                for b in range(PB):
                    need(dve, z_ok, pair, 2 * ln + 1 + b)
                    for k in (T * b, T * b + 1):
                        last = dve.bn_stats(bnst[:, k, :], zs[ln % 2][:, k, :])
                last.then_inc(stats_ok.sem, 1)
                need_apart(dve, stats_ok, pair, ln + 1)
                for k in range(KT):
                    last = dve.bn_aggr(mv[:, k, :], bnst[:, k, :])
                last.then_inc(mv_ok.sem, 1)
                need(dve, mv_ok, pair, ln + 1)
                dve.tensor_scalar(vareps[:, :], mv[:, :, 1], EPS, None, ALU.add)
                dve.tensor_scalar(negmean[:, :], mv[:, :, 0], -1.0, None, ALU.mult).then_inc(var_ok.sem, 1)

            def after_attention(pair, a):
                if a == H2T_LO_SLOT:
                    for c in range(EC):
                        need(dve, h2T_hi_ok, pair, c + 1)
                        dve.tensor_tensor(out=h2T_lo[:, c, :], in0=ps_tail[c][:, :],
                                          in1=h2T_hi[:, c, :].bitcast(F32), op=ALU.subtract)\
                            .then_inc(h2T_lo_ok.sem, 1)
                if a in FFN_READ_SLOT:
                    b = FFN_READ_SLOT[a]
                    need(dve, mm_ffn, pair, b + 1)
                    for k in (T * b, T * b + 1):
                        last = dve.scalar_tensor_tensor(
                            out=zs[0][:, k, :], in0=ps_tail[b][:, (k % T) * E:(k % T + 1) * E],
                            scalar=fscale[:, 0:1], in1=h2[:, k, :], op0=ALU.mult, op1=ALU.add)
                    last.then_inc(z_ok.sem, 1)
                if a in DIVIDE_SLOT:
                    for k in DIVIDE_SLOT[a]:
                        need(dve, mm_y, pair, k + 1)
                        y3 = ps_tail[k % 2][:, :].rearrange("p (h d) -> p h d", d=HW)
                        dve.reciprocal(rden[:, k, :].unsqueeze(2), y3[:, :, DH:DH + 1])\
                            .then_inc(rden_ok.sem, 1)
                        need(dve, rden_ok, pair, k + 1)
                        dve.tensor_tensor(out=yn[:, k, :].rearrange("p (h d) -> p h d", d=DH),
                                          in0=y3[:, :, 0:DH],
                                          in1=rden[:, k, :].unsqueeze(2).to_broadcast([P, HEADS, DH]),
                                          op=ALU.mult).then_inc(yn_ok.sem, 1)
                if a == YNT_LO_SLOT:
                    for c in range(EC):
                        need(dve, ynT_hi_ok, pair, c + 1)
                        dve.tensor_tensor(out=ynT_lo[:, c, :], in0=ps_tail[c][:, :],
                                          in1=ynT_hi[:, c, :].bitcast(F32), op=ALU.subtract)\
                            .then_inc(ynT_lo_ok.sem, 1)
                if a in PROJ_READ_SLOT:
                    b = PROJ_READ_SLOT[a]
                    need(dve, mm_proj, pair, b + 1)
                    need(dve, xres_ok, pair, 1)
                    need(dve, norm_ok, pair - 1, 6)
                    dve.tensor_tensor(out=zs[0][:, T * b:T * b + T, :].rearrange("p t e -> p (t e)"),
                                      in0=ps_tail[b][:, :],
                                      in1=xres[:, T * b:T * b + T, :].rearrange("p t e -> p (t e)"),
                                      op=ALU.add).then_inc(z_ok.sem, 1)
                if a == SCORE_MAX_SLOT:
                    need(dve, mm_sc, pair, 1)
                    dve.tensor_tensor(out=sc[:, :, :],
                                      in0=ps_tail[0][:, 0:KT * CP].rearrange("p (k c) -> p k c", c=CP)[:, :, 0:C],
                                      in1=xmask[:, :, :], op=ALU.add).then_inc(sc_ok.sem, 1)
                    need(dve, sc_ok, pair, 1)
                    dve.tensor_reduce(nmx[:, :], sc[:, :, :], axis=AX.X, op=ALU.max, negate=True)\
                        .then_inc(nmx_ok.sem, 1)
                if a == RSUM_SLOT:
                    need(dve, p2_ok, pair, 1)
                    dve.reciprocal(rsum[:, :], ssum[:, :]).then_inc(rsum_ok.sem, 1)
                if a in XAV_READ_SLOT:
                    need(dve, rsum_ok, pair, 1)
                    for b in XAV_READ_SLOT[a]:
                        need(dve, mm_xav, pair, b + 1)
                        for k in (T * b, T * b + 1):
                            last = dve.scalar_tensor_tensor(
                                out=zs[1][:, k, :], in0=ps_tail[b][:, (k % T) * E:(k % T + 1) * E],
                                scalar=rsum[:, k:k + 1], in1=h1[:, k, :], op0=ALU.mult, op1=ALU.add)
                        last.then_inc(z_ok.sem, 1)
                if a in STATS_SLOT:
                    statistics(pair, STATS_SLOT[a])

            def iteration(p, load=False, head=False, main=False, tail=False, late=False):
                for s in range(SLOTS):
                    unit = max_unit(p, s, main, head)
                    if unit:
                        pair, n = unit
                        q, b, u = n // 6, n // 3 % 2, n % 3
                        need(dve, mm_max, pair, n + 1)
                        if n % 6 == 0:
                            need(dve, negmax_ok, pair, q - 1)
                        dve.tensor_reduce(rowmax2[:, q % 2, b, :] if u == 2 else rowmax[:, q % 2, b, u, :],
                                          ps_max[n % 2][:, :].rearrange("p (j c) -> p j c", c=P),
                                          axis=AX.X, op=ALU.max, negate=True).then_inc(max_ok.sem, 1)
                        if n % 6 == 5:
                            need(dve, max_ok, pair, n + 1)
                            m = rowmax[:, q % 2, :, 1, :]
                            dve.tensor_tensor(out=m, in0=m, in1=rowmax2[:, q % 2], op=ALU.min)\
                                .then_inc(max2_ok.sem, 1)
                    for t in (s, s + 0.5):
                        for pair, a in stages(p, t, tail, late):
                            after_attention(pair, a)
                        if t in XT_LO_SLOT and head:
                            c = XT_LO_SLOT[t]
                            need(dve, xT_hi_ok, p + 1, c + 1)
                            dve.tensor_tensor(out=xT_lo[:, c, :], in0=ps_head[:, :],
                                              in1=xT_hi[:, c, :].bitcast(F32), op=ALU.subtract)\
                                .then_inc(xT_lo_ok.sem, 1)
                        if t in QK_REST_SLOT and head:
                            c, i = QK_REST_SLOT[t]
                            n = 2 * c + i + 1
                            need(dve, qk_hi_ok, p + 1, n)
                            need(dve, low_ok, p + 1, n - 2)
                            dve.scalar_tensor_tensor(out=rest[:, i, :], in0=ps_head[:, :], scalar=bqk[:, i, c:c + 1],
                                                     in1=parts[i][:, c, HI[i], :], op0=ALU.add, op1=ALU.subtract)\
                                .then_inc(rest_ok.sem, 1)
                            dve.tensor_copy(parts[i][:, c, HI_COPIES[i], :],
                                            parts[i][:, c, HI[i]:HI[i] + 1, :].to_broadcast([P, 2, TOK]))\
                                .then_inc(copies_ok.sem, 1)

            run(dve, iteration)

        @block.tensor
        def _(pe):
            def three_passes(dst, st_hi, st_lo, mv_hi, mv_lo, chunks):
                n = 0
                for c in range(chunks):
                    for a, m in ((st_hi, mv_hi), (st_hi, mv_lo), (st_lo, mv_hi)):
                        last = pe.matmul(dst, a(c), m(c), start=(n == 0), stop=(n == 3 * chunks - 1))
                        n += 1
                return last

            pe.wait_ge(cst, 9)
            pe.wait_ge(vcst, 4)
            pe.matmul(ps_av[:, 0:1], ones[:, :], wf_abs[:, :], start=True, stop=True).then_inc(prep_mm, 1)
            pe.wait_ge(w_in.sem, W_IN)

            def transpose_weights(i, src):
                dst = ps_tail[0] if i % 2 else ps_head
                for ci in range(EC):
                    for co in range(EC):
                        last = pe.transpose(dst[:, ci * E + co * P:ci * E + co * P + P],
                                            src[:, co, ci * P:(ci + 1) * P], ident[:, :])
                last.then_inc(prep_mm, 1)

            for i in range(4):
                if i >= 2:
                    pe.wait_ge(prep_lo, i - 1)
                transpose_weights(i, w_raw[:, i])
            pe.wait_ge(vcst, 12)
            pe.wait_ge(prep_lo, 4)
            transpose_weights(4, wf_q)
            n = 0
            for c in range(EC):
                for part in (wT_hi[3], wT_lo[3]):
                    pe.matmul(ps_av[:, 0:E], bv_bc[:, c, :], part[:, c, :].bitcast(F32), start=(n == 0), stop=False)
                    n += 1
            pe.matmul(ps_av[:, 0:E], ones[0:1, :], bp_row[:, :], start=False, stop=True).then_inc(prep_mm, 1)
            pe.wait_ge(prep_hi, 5)
            pe.wait_ge(prep_lo, 5)

            def after_attention(pair, a):
                if a in FFN_SLOT:
                    b = FFN_SLOT[a]
                    need(pe, h2T_lo_ok, pair, 2)
                    for t in range(T):
                        tok = slice((T * b + t) * P, (T * b + t + 1) * P)
                        n = 0
                        for c in range(EC):
                            for part in (h2T_hi, h2T_lo):
                                last = pe.matmul(ps_tail[b][:, t * E:(t + 1) * E], part[:, c, tok], wfT[:, c, :],
                                                 start=(n == 0), stop=(n == 2 * EC - 1))
                                n += 1
                    last.then_inc(mm_ffn.sem, 1)
                if a in HEADS_SLOT:
                    for k in HEADS_SLOT[a]:
                        b, t = k // T, k % T
                        if k == 0:
                            need(pe, y_ok, pair, 4)
                        if k < 2:
                            need(pe, z_ok, pair - 1, 5 + k)
                        else:
                            need(pe, yn_ok, pair, k - 1)
                        for q in range(QUADS):
                            last = pe.transpose(ps_tail[k % 2][:, q * P:(q + 1) * P],
                                                y_sb[:, q, b, t * P:(t + 1) * P], ident[:, :])
                        last.then_inc(mm_y.sem, 1)
                if a == YNT_SLOT:
                    need(pe, yn_ok, pair, 4)
                    for c in range(EC):
                        for k in range(KT):
                            last = pe.transpose(ps_tail[c][:, k * P:(k + 1) * P], yn[:, k, c * P:(c + 1) * P],
                                                ident[:, :])
                        last.then_inc(mm_ynT.sem, 1)
                if a in PROJ_SLOT:
                    b = PROJ_SLOT[a]
                    need(pe, ynT_lo_ok, pair, 2)
                    for t in range(T):
                        tok = slice((T * b + t) * P, (T * b + t + 1) * P)
                        last = three_passes(ps_tail[b][:, t * E:(t + 1) * E],
                                            lambda c: ynT_hi[:, c, tok], lambda c: ynT_lo[:, c, tok],
                                            lambda c: wT_hi[3][:, c, :], lambda c: wT_lo[3][:, c, :], EC)
                    last.then_inc(mm_proj.sem, 1)
                if a == CTXT_SLOT:
                    need(pe, ctx_landed, pair, 1)
                    need(pe, z_ok, pair, 1)
                    for b in range(PB):
                        for c in range(EC):
                            n = b * EC + c
                            last = pe.transpose(ps_tail[0][:, n * CP:n * CP + C],
                                                ctx_sb[:, b, c * P:(c + 1) * P], ident[0:C, 0:C])
                    last.then_inc(mm_ctxT.sem, 1)
                if a == H1T_SLOT:
                    need(pe, norm_ok, pair, 2)
                    need(pe, ctxT_ok, pair, 1)
                    for c in range(EC):
                        for k in range(KT):
                            last = pe.transpose(ps_tail[c][:, k * P:(k + 1) * P], h1[:, k, c * P:(c + 1) * P],
                                                ident[:, :])
                        last.then_inc(mm_h1T.sem, 1)
                if a == SCORE_SLOT:
                    need(pe, h1T_ok, pair, 2)
                    for k in range(KT):
                        for c in range(EC):
                            last = pe.matmul(ps_tail[0][:, k * CP:k * CP + C], h1T[:, c, k * P:(k + 1) * P],
                                             ctxT[:, (k // T) * EC + c, 0:C], start=(c == 0), stop=(c == EC - 1))
                    last.then_inc(mm_sc.sem, 1)
                if a == PT_SLOT:
                    need(pe, p2_ok, pair, 1)
                    for k in range(KT):
                        last = pe.transpose(ps_tail[1][0:C, k * P:(k + 1) * P], p2[:, k, :], ident[:, :])
                    last.then_inc(mm_pT.sem, 1)
                if a == XAV_SLOT:
                    need(pe, p2T_ok, pair, 1)
                    for b in range(PB):
                        for t in range(T):
                            k = T * b + t
                            last = pe.matmul(ps_tail[b][:, t * E:(t + 1) * E], p2T[:, k * P:(k + 1) * P],
                                             ctx_sb[:, b, :], start=True, stop=True)
                        last.then_inc(mm_xav.sem, 1)
                if a == H2T_SLOT:
                    need(pe, norm_ok, pair, 4)
                    for c in range(EC):
                        for k in range(KT):
                            last = pe.transpose(ps_tail[c][:, k * P:(k + 1) * P], h2[:, k, c * P:(c + 1) * P],
                                                ident[:, :])
                        last.then_inc(mm_h2T.sem, 1)

            def iteration(p, load=False, head=False, main=False, tail=False, late=False):
                for s in range(SLOTS):
                    if main:
                        q, b, u = s // 6, s // 3 % 2, s % 3
                        if s % 6 == 0:
                            need(pe, mrow_in[q], p, 1)
                        need(pe, exp_ok, p, s - 1)
                        t0 = b * S
                        for j in (range(4) if u == 2 else range(2 * u, 2 * u + 2)):
                            h = 4 * q + j
                            if u == 2:
                                keys, queries, at = slice(t0 + P, t0 + S), slice(t0 + P, t0 + S), P * j
                            else:
                                keys, queries, at = slice(t0, t0 + P), slice(t0, t0 + S), S * (j % 2)
                            last = pe.matmul(ps_st[s % 2][:, at:at + queries.stop - queries.start],
                                             stack[1][0:KROWS + 2, h, keys], stack[0][0:KROWS + 2, h, queries],
                                             start=True, stop=True)
                        last.then_inc(mm_st.sem, 1)
                    unit = max_unit(p, s, main, head)
                    if unit:
                        pair, n = unit
                        q, b, u = n // 6, n // 3 % 2, n % 3
                        if n % 6 == 0:
                            for i in range(2):
                                need(pe, stack_in[q][i], pair, 4)
                        need(pe, max_ok, pair, n - 1)
                        t0 = b * S
                        queries = slice(t0, t0 + P) if u == 0 else slice(t0 + P, t0 + S)
                        keys = slice(t0 + P, t0 + S) if u == 2 else slice(t0, t0 + P)
                        if u != 1:
                            pe.matmul(ps_max[n % 2][:, :], ident_b[:, :],
                                      causal_b[:, :, :].rearrange("p j c -> p (j c)"), start=True, stop=False)
                        for j in range(4):
                            h = 4 * q + j
                            last = pe.matmul(ps_max[n % 2][:, P * j:P * j + P], stack[0][0:KROWS, h, queries],
                                             stack[1][0:KROWS, h, keys], start=(u == 1), stop=(u == 1 or j == 3))
                        last.then_inc(mm_max.sem, 1)
                    av = {5: (0, 0), 8: (0, 1), 11: (1, 0), 14: (1, 1), 17: (2, 0), 20: (2, 1), 23: (3, 0),
                          2: (3, 1)}.get(s)
                    if av and (tail if s == 2 else main):
                        q, b = av
                        pair = p - (s == 2)
                        need(pe, sel_ok, pair, 6 * q + 3 * b + 3)
                        if q == 0:
                            need(pe, v_ok, pair, b + 1)
                        if b == 0:
                            need(pe, y_ok, pair, q)
                            if q < 3 or head:
                                need(pe, mT_ok, pair, q + 2)
                        for kb in range(T):
                            for j in range(4):
                                if kb == 0:
                                    pr = probs[:, q % 2, 3 * b + j // 2, S * (j % 2):S * (j % 2) + S]
                                else:
                                    pr = probs[:, q % 2, 3 * b + 2, P * j:P * j + P]
                                last = pe.matmul(ps_av[HW * j:HW * j + HW, b * S + kb * P:b * S + S],
                                                 v_ext[:, T * b + kb, 4 * q + j, :], pr,
                                                 start=(kb == 0), stop=(kb == 1), skip_group_check=True,
                                                 tile_position=(0, HW * j))
                        last.then_inc(mm_av.sem, 1)
                    if s in MT_SLOT and (main if MT_SLOT[s] else head):
                        q, pair = MT_SLOT[s], p + (MT_SLOT[s] == 0)
                        need(pe, negmax_ok, pair, q + 1)
                        need(pe, y_ok, pair, q - 1)
                        for b in range(PB):
                            for t in range(T):
                                at = (T * b + t) * P
                                last = pe.transpose(ps_av[:, :].bitcast(BF16)[0:8, at:at + P],
                                                    negmax[:, b, t, :, :].rearrange("p i j -> p (i j)"), ident_b[:, :])
                        last.then_inc(mm_mT.sem, 1)
                    for t in (s, s + 0.5):
                        for pair, a in stages(p, t, tail, late):
                            after_attention(pair, a)
                        if t in XT_SLOT and head:
                            c = XT_SLOT[t]
                            if c == 0:
                                need(pe, x_in, p + 1, 1)
                                need(pe, v_ok, p, 2)
                            else:
                                need(pe, xT_lo_ok, p + 1, 1)
                            for k in range(KT):
                                last = pe.transpose(ps_head[:, k * P:(k + 1) * P], xt[:, k, c * P:(c + 1) * P],
                                                    ident[:, :])
                            last.then_inc(mm_xT.sem, 1)
                        if t in QK_SLOT and head:
                            c, i = QK_SLOT[t]
                            n = 2 * c + i + 1
                            if n == 1:
                                need(pe, xT_lo_ok, p + 1, 2)
                            else:
                                need(pe, rest_ok, p + 1, n - 1)
                            out_c = slice(c * P, (c + 1) * P)
                            three_passes(ps_head[:, :],
                                         lambda k: wT_hi[i][:, k, out_c], lambda k: wT_lo[i][:, k, out_c],
                                         lambda k: xT_hi[:, k, :], lambda k: xT_lo[:, k, :], EC)\
                                .then_inc(mm_qk.sem, 1)
                        if t in V_SLOT and main:
                            b = V_SLOT[t]
                            if b == 0:
                                need(pe, rest_ok, p, 4)
                            else:
                                need(pe, v_ok, p, 1)
                            for tile in range(T):
                                tok = slice((T * b + tile) * P, (T * b + tile + 1) * P)
                                last = three_passes(ps_head[:, tile * E:(tile + 1) * E],
                                                    lambda c: xT_hi[:, c, tok], lambda c: xT_lo[:, c, tok],
                                                    lambda c: wT_hi[2][:, c, :], lambda c: wT_lo[2][:, c, :], EC)
                            last.then_inc(mm_v.sem, 1)

            run(pe, iteration)


_INS = ["x", "ctx_1024", "L0_attn_Wq", "L0_attn_bq", "L0_attn_Wk", "L0_attn_bk", "L0_attn_Wv", "L0_attn_bv",
        "L0_attn_Wp", "L0_attn_bp", "L0_ffn_weight"]


def kernel(**inputs):
    import numpy as _np
    import concourse.bacc as _bacc
    from concourse import mybir as _mybir
    from concourse.bass_utils import run_bass_kernel_spmd as _run

    nc = _bacc.Bacc("TRN2", target_bir_lowering=False, num_devices=1)
    arrays, args = {}, []
    for name in _INS:
        a = _np.ascontiguousarray(inputs[name])
        arrays[f"in_{name}"] = a
        args.append(nc.dram_tensor(f"in_{name}", a.shape, _mybir.dt.from_np(a.dtype), kind="ExternalInput").ap())
    shape = inputs["x"].shape
    args.append(nc.dram_tensor("out_0", shape, _mybir.dt.float32, kind="ExternalOutput").ap())
    decoder_layer(nc, *args)
    r = _run(nc, [arrays], core_ids=[0])
    return r.results[0]["out_0"]
```
